# Optimizing a Trainium2 kernel written in Bass

```python
import numpy as np
import jax
import jax.numpy as jnp

def _softmax(x, axis=-1):
    return jax.nn.softmax(x, axis=axis)

def _gelu(x):
    return jax.nn.gelu(x, approximate=True)

def _silu(x):
    return jax.nn.silu(x)

def _sigmoid(x):
    return jax.nn.sigmoid(x)

def _layernorm(x, axis=-1, eps=1e-05):
    m = jnp.mean(x, axis=axis, keepdims=True)
    v = jnp.var(x, axis=axis, keepdims=True)
    return (x - m) / jnp.sqrt(v + eps)

def _scatter_add(tgt, idx, src, axis=0):
    return tgt.at[idx].add(src)

def _segment_sum(src, seg, n):
    return jax.ops.segment_sum(src, seg, n)
kernel_name = 'mk_xattn_seq_d2_seqx_r8_94ce6d'

def setup_inputs(seed: int=0):
    np.random.seed(seed)
    _w = jnp.asarray

    def _rec_inputs():
        import jax
        import jax.numpy as jnp
        _rk = jax.random.key(seed)
        x = -0.0003929 + 0.9999 * jax.random.normal(jax.random.fold_in(_rk, 1), (4, 256, 256), jnp.float32)
        _lenS = 256 - jax.random.randint(jax.random.fold_in(_rk, 7), (4,), 0, max(1, 256 // 4) + 1, jnp.int32)
        _lenS2 = 256 - jax.random.randint(jax.random.fold_in(_rk, 8), (4,), 0, max(1, 256 // 4) + 1, jnp.int32)
        _ctx_2048P = jax.random.normal(jax.random.fold_in(_rk, 11), (4, 16, 256), jnp.float32)
        _ctx_2048c = jax.random.dirichlet(jax.random.fold_in(_rk, 511), 0.3 * jnp.ones((16,), jnp.float32), (4, 256))
        _ctx_2048t = jnp.einsum('bsk,bkd->bsd', _ctx_2048c, _ctx_2048P)
        _ctx_2048t = _ctx_2048t * jax.lax.rsqrt(jnp.mean(jnp.square(_ctx_2048t)) + 1e-12) * 0.953939
        ctx_2048 = -8.57375e-05 + 0.999917 * (_ctx_2048t + 0.3 * jax.random.normal(jax.random.fold_in(_rk, 611), (4, 256, 256), jnp.float32))
        _validS = jnp.arange(256)[None, :] < _lenS[:, None]
        _validS2 = jnp.arange(256)[None, :] < _lenS2[:, None]
        _causal = jnp.tril(jnp.ones((256, 256), dtype=bool))
        mask_BxS2_bf1 = jnp.ones((4, 256), dtype=bool)
        return (x, ctx_2048, mask_BxS2_bf1)
    x, ctx_2048, mask_BxS2_bf1 = _rec_inputs()

    def _L0_xattn_setup():
        import jax, jax.numpy as jnp
        import numpy as np
        HIDDEN = 256
        HEADS = 16
        HEAD_DIM = HIDDEN // HEADS
        LN_EPS = 1e-05
        GATE_INIT = 0.5

        def _layer_norm(x, gamma, beta):
            mu = jnp.mean(x, axis=-1, keepdims=True)
            var = jnp.mean(jnp.square(x - mu), axis=-1, keepdims=True)
            return (x - mu) * jax.lax.rsqrt(var + LN_EPS) * gamma + beta
        key = jax.random.key(seed)
        ks = jax.random.split(key, 8)
        B, T_TEXT, T_AUDIO = (4, 256, 1500)
        s = 0.02
        return {'hidden_states': jax.random.normal(ks[0], (B, T_TEXT, HIDDEN), jnp.float32), 'audio_kv': jax.random.normal(ks[1], (B, T_AUDIO, HIDDEN), jnp.float32), 'audio_attention_mask': jnp.ones((B, T_AUDIO), dtype=bool), 'Wq': jax.random.normal(ks[2], (HIDDEN, HIDDEN), jnp.float32) * s, 'Wk': jax.random.normal(ks[3], (HIDDEN, HIDDEN), jnp.float32) * s, 'Wv': jax.random.normal(ks[4], (HIDDEN, HIDDEN), jnp.float32) * s, 'Wo': jax.random.normal(ks[5], (HIDDEN, HIDDEN), jnp.float32) * s, 'ln_gamma': jnp.ones((HIDDEN,), jnp.float32), 'ln_beta': jnp.zeros((HIDDEN,), jnp.float32), 'gate': jnp.array([GATE_INIT], jnp.float32)}
    _L0_xattn_all = _L0_xattn_setup()
    _L0_xattn_in = {k: v for k, v in _L0_xattn_all.items() if k in ('Wq', 'Wk', 'Wv', 'Wo', 'ln_gamma', 'ln_beta', 'gate')}
    del _L0_xattn_all

    def _L1_xattn_setup():
        import jax, jax.numpy as jnp
        import numpy as np
        B, Q, S1, S2 = (4, 32, 256, 256)
        D, H, K, F = (256, 16, 128, 1024)
        LN_EPS = 1e-05

        def _layer_norm(x, scale, offset):
            mu = jnp.mean(x, axis=-1, keepdims=True)
            var = jnp.var(x, axis=-1, keepdims=True)
            return (x - mu) * jax.lax.rsqrt(var + LN_EPS) * scale + offset

        def _cross_attention(q_in, kv_in, wq, bq, wk, bk, wv, bv, wo, bo, bias_k, bias_v):
            b, q_len, _ = q_in.shape
            t = kv_in.shape[1]
            qh = (q_in @ wq + bq).reshape(b, q_len, H, K)
            kh = (kv_in @ wk + bk).reshape(b, t, H, K)
            vh = (kv_in @ wv + bv).reshape(b, t, H, K)
            kh = jnp.concatenate([kh, jnp.broadcast_to(bias_k, (b, 1, H, K))], axis=1)
            vh = jnp.concatenate([vh, jnp.broadcast_to(bias_v, (b, 1, H, K))], axis=1)
            scale = jnp.sqrt(jnp.asarray(K, q_in.dtype))
            logits = jnp.einsum('bqhk,bthk->bhqt', qh, kh) / scale
            weights = jax.nn.softmax(logits, axis=-1)
            ctx = jnp.einsum('bhqt,bthk->bqhk', weights, vh).reshape(b, q_len, H * K)
            return ctx @ wo + bo

        def _forward(x, xf_1, xf_2, ln1_scale, ln1_offset, wq1, bq1, wk1, bk1, wv1, bv1, wo1, bo1, bias_k1, bias_v1, ln2_scale, ln2_offset, wq2, bq2, wk2, bk2, wv2, bv2, wo2, bo2, bias_k2, bias_v2, ln_mlp_scale, ln_mlp_offset, w_fc1, b_fc1, w_fc2, b_fc2):
            res = x
            h = _layer_norm(x, ln1_scale, ln1_offset)
            x = res + _cross_attention(h, xf_1, wq1, bq1, wk1, bk1, wv1, bv1, wo1, bo1, bias_k1, bias_v1)
            res = x
            h = _layer_norm(x, ln2_scale, ln2_offset)
            x = res + _cross_attention(h, xf_2, wq2, bq2, wk2, bk2, wv2, bv2, wo2, bo2, bias_k2, bias_v2)
            h = _layer_norm(x, ln_mlp_scale, ln_mlp_offset)
            h = jax.nn.gelu(h @ w_fc1 + b_fc1, approximate=False) @ w_fc2 + b_fc2
            return x + h
        key = jax.random.key(seed)
        ks = iter(jax.random.split(key, 64))

        def rn(shape, s=0.02):
            return jax.random.normal(next(ks), shape, jnp.float32) * s
        inp = {'x': rn((B, Q, D), 1.0), 'xf_1': rn((B, S1, D), 1.0), 'xf_2': rn((B, S2, D), 1.0)}
        for i in (1, 2):
            inp[f'ln{i}_scale'] = jnp.ones((D,), jnp.float32)
            inp[f'ln{i}_offset'] = jnp.zeros((D,), jnp.float32)
            inp[f'wq{i}'] = rn((D, H * K))
            inp[f'bq{i}'] = jnp.zeros((H * K,), jnp.float32)
            inp[f'wk{i}'] = rn((D, H * K))
            inp[f'bk{i}'] = jnp.zeros((H * K,), jnp.float32)
            inp[f'wv{i}'] = rn((D, H * K))
            inp[f'bv{i}'] = jnp.zeros((H * K,), jnp.float32)
            inp[f'wo{i}'] = rn((H * K, D))
            inp[f'bo{i}'] = jnp.zeros((D,), jnp.float32)
            inp[f'bias_k{i}'] = rn((1, 1, H, K))
            inp[f'bias_v{i}'] = rn((1, 1, H, K))
        inp['ln_mlp_scale'] = jnp.ones((D,), jnp.float32)
        inp['ln_mlp_offset'] = jnp.zeros((D,), jnp.float32)
        inp['w_fc1'] = rn((D, F))
        inp['b_fc1'] = jnp.zeros((F,), jnp.float32)
        inp['w_fc2'] = rn((F, D))
        inp['b_fc2'] = jnp.zeros((D,), jnp.float32)
        return inp
    _L1_xattn_all = _L1_xattn_setup()
    _L1_xattn_in = {k: v for k, v in _L1_xattn_all.items() if k in ('ln1_scale', 'ln1_offset', 'wq1', 'bq1', 'wk1', 'bk1', 'wv1', 'bv1', 'wo1', 'bo1', 'bias_k1', 'bias_v1', 'ln2_scale', 'ln2_offset', 'wq2', 'bq2', 'wk2', 'bk2', 'wv2', 'bv2', 'wo2', 'bo2', 'bias_k2', 'bias_v2', 'ln_mlp_scale', 'ln_mlp_offset', 'w_fc1', 'b_fc1', 'w_fc2', 'b_fc2')}
    del _L1_xattn_all
    return {'x': x, 'ctx_2048': ctx_2048, 'mask_BxS2_bf1': mask_BxS2_bf1, 'L0_xattn_Wq': _L0_xattn_in['Wq'], 'L0_xattn_Wk': _L0_xattn_in['Wk'], 'L0_xattn_Wv': _L0_xattn_in['Wv'], 'L0_xattn_Wo': _L0_xattn_in['Wo'], 'L0_xattn_ln_gamma': _L0_xattn_in['ln_gamma'], 'L0_xattn_ln_beta': _L0_xattn_in['ln_beta'], 'L0_xattn_gate': _L0_xattn_in['gate'], 'L1_xattn_ln1_scale': _L1_xattn_in['ln1_scale'], 'L1_xattn_ln1_offset': _L1_xattn_in['ln1_offset'], 'L1_xattn_wq1': _L1_xattn_in['wq1'], 'L1_xattn_bq1': _L1_xattn_in['bq1'], 'L1_xattn_wk1': _L1_xattn_in['wk1'], 'L1_xattn_bk1': _L1_xattn_in['bk1'], 'L1_xattn_wv1': _L1_xattn_in['wv1'], 'L1_xattn_bv1': _L1_xattn_in['bv1'], 'L1_xattn_wo1': _L1_xattn_in['wo1'], 'L1_xattn_bo1': _L1_xattn_in['bo1'], 'L1_xattn_bias_k1': _L1_xattn_in['bias_k1'], 'L1_xattn_bias_v1': _L1_xattn_in['bias_v1'], 'L1_xattn_ln2_scale': _L1_xattn_in['ln2_scale'], 'L1_xattn_ln2_offset': _L1_xattn_in['ln2_offset'], 'L1_xattn_wq2': _L1_xattn_in['wq2'], 'L1_xattn_bq2': _L1_xattn_in['bq2'], 'L1_xattn_wk2': _L1_xattn_in['wk2'], 'L1_xattn_bk2': _L1_xattn_in['bk2'], 'L1_xattn_wv2': _L1_xattn_in['wv2'], 'L1_xattn_bv2': _L1_xattn_in['bv2'], 'L1_xattn_wo2': _L1_xattn_in['wo2'], 'L1_xattn_bo2': _L1_xattn_in['bo2'], 'L1_xattn_bias_k2': _L1_xattn_in['bias_k2'], 'L1_xattn_bias_v2': _L1_xattn_in['bias_v2'], 'L1_xattn_ln_mlp_scale': _L1_xattn_in['ln_mlp_scale'], 'L1_xattn_ln_mlp_offset': _L1_xattn_in['ln_mlp_offset'], 'L1_xattn_w_fc1': _L1_xattn_in['w_fc1'], 'L1_xattn_b_fc1': _L1_xattn_in['b_fc1'], 'L1_xattn_w_fc2': _L1_xattn_in['w_fc2'], 'L1_xattn_b_fc2': _L1_xattn_in['b_fc2']}

def reference(x, ctx_2048, mask_BxS2_bf1, L0_xattn_Wq, L0_xattn_Wk, L0_xattn_Wv, L0_xattn_Wo, L0_xattn_ln_gamma, L0_xattn_ln_beta, L0_xattn_gate, L1_xattn_ln1_scale, L1_xattn_ln1_offset, L1_xattn_wq1, L1_xattn_bq1, L1_xattn_wk1, L1_xattn_bk1, L1_xattn_wv1, L1_xattn_bv1, L1_xattn_wo1, L1_xattn_bo1, L1_xattn_bias_k1, L1_xattn_bias_v1, L1_xattn_ln2_scale, L1_xattn_ln2_offset, L1_xattn_wq2, L1_xattn_bq2, L1_xattn_wk2, L1_xattn_bk2, L1_xattn_wv2, L1_xattn_bv2, L1_xattn_wo2, L1_xattn_bo2, L1_xattn_bias_k2, L1_xattn_bias_v2, L1_xattn_ln_mlp_scale, L1_xattn_ln_mlp_offset, L1_xattn_w_fc1, L1_xattn_b_fc1, L1_xattn_w_fc2, L1_xattn_b_fc2):
    import jax
    import jax.numpy as jnp

    def _L0_xattn_ref(hidden_states, audio_kv, audio_attention_mask, Wq, Wk, Wv, Wo, ln_gamma, ln_beta, gate):
        import jax, jax.numpy as jnp
        import numpy as np
        HIDDEN = 256
        HEADS = 16
        HEAD_DIM = HIDDEN // HEADS
        LN_EPS = 1e-05
        GATE_INIT = 0.5

        def _layer_norm(x, gamma, beta):
            mu = jnp.mean(x, axis=-1, keepdims=True)
            var = jnp.mean(jnp.square(x - mu), axis=-1, keepdims=True)
            return (x - mu) * jax.lax.rsqrt(var + LN_EPS) * gamma + beta
        B, Tt, D = hidden_states.shape
        Ta = audio_kv.shape[1]
        scale = HEAD_DIM ** (-0.5)
        a = _layer_norm(audio_kv, ln_gamma, ln_beta)
        Q = (hidden_states @ Wq.T).reshape(B, Tt, HEADS, HEAD_DIM).transpose(0, 2, 1, 3)
        K = (a @ Wk.T).reshape(B, Ta, HEADS, HEAD_DIM).transpose(0, 2, 1, 3)
        V = (a @ Wv.T).reshape(B, Ta, HEADS, HEAD_DIM).transpose(0, 2, 1, 3)
        scores = jnp.einsum('bhtd,bhsd->bhts', Q, K) * scale
        mask = audio_attention_mask[:, None, None, :]
        scores = jnp.where(mask, scores, jnp.float32(-jnp.inf))
        attn = jax.nn.softmax(scores, axis=-1)
        out = jnp.einsum('bhts,bhsd->bhtd', attn, V)
        out = out.transpose(0, 2, 1, 3).reshape(B, Tt, D)
        out = out @ Wo.T
        return hidden_states + jnp.tanh(gate) * out

    def _L1_xattn_ref(x, xf_1, xf_2, ln1_scale, ln1_offset, wq1, bq1, wk1, bk1, wv1, bv1, wo1, bo1, bias_k1, bias_v1, ln2_scale, ln2_offset, wq2, bq2, wk2, bk2, wv2, bv2, wo2, bo2, bias_k2, bias_v2, ln_mlp_scale, ln_mlp_offset, w_fc1, b_fc1, w_fc2, b_fc2):
        import jax, jax.numpy as jnp
        import numpy as np
        B, Q, S1, S2 = (4, 32, 256, 256)
        D, H, K, F = (256, 16, 128, 1024)
        LN_EPS = 1e-05

        def _layer_norm(x, scale, offset):
            mu = jnp.mean(x, axis=-1, keepdims=True)
            var = jnp.var(x, axis=-1, keepdims=True)
            return (x - mu) * jax.lax.rsqrt(var + LN_EPS) * scale + offset

        def _cross_attention(q_in, kv_in, wq, bq, wk, bk, wv, bv, wo, bo, bias_k, bias_v):
            b, q_len, _ = q_in.shape
            t = kv_in.shape[1]
            qh = (q_in @ wq + bq).reshape(b, q_len, H, K)
            kh = (kv_in @ wk + bk).reshape(b, t, H, K)
            vh = (kv_in @ wv + bv).reshape(b, t, H, K)
            kh = jnp.concatenate([kh, jnp.broadcast_to(bias_k, (b, 1, H, K))], axis=1)
            vh = jnp.concatenate([vh, jnp.broadcast_to(bias_v, (b, 1, H, K))], axis=1)
            scale = jnp.sqrt(jnp.asarray(K, q_in.dtype))
            logits = jnp.einsum('bqhk,bthk->bhqt', qh, kh) / scale
            weights = jax.nn.softmax(logits, axis=-1)
            ctx = jnp.einsum('bhqt,bthk->bqhk', weights, vh).reshape(b, q_len, H * K)
            return ctx @ wo + bo

        def _forward(x, xf_1, xf_2, ln1_scale, ln1_offset, wq1, bq1, wk1, bk1, wv1, bv1, wo1, bo1, bias_k1, bias_v1, ln2_scale, ln2_offset, wq2, bq2, wk2, bk2, wv2, bv2, wo2, bo2, bias_k2, bias_v2, ln_mlp_scale, ln_mlp_offset, w_fc1, b_fc1, w_fc2, b_fc2):
            res = x
            h = _layer_norm(x, ln1_scale, ln1_offset)
            x = res + _cross_attention(h, xf_1, wq1, bq1, wk1, bk1, wv1, bv1, wo1, bo1, bias_k1, bias_v1)
            res = x
            h = _layer_norm(x, ln2_scale, ln2_offset)
            x = res + _cross_attention(h, xf_2, wq2, bq2, wk2, bk2, wv2, bv2, wo2, bo2, bias_k2, bias_v2)
            h = _layer_norm(x, ln_mlp_scale, ln_mlp_offset)
            h = jax.nn.gelu(h @ w_fc1 + b_fc1, approximate=False) @ w_fc2 + b_fc2
            return x + h
        return _forward(x, xf_1, xf_2, ln1_scale, ln1_offset, wq1, bq1, wk1, bk1, wv1, bv1, wo1, bo1, bias_k1, bias_v1, ln2_scale, ln2_offset, wq2, bq2, wk2, bk2, wv2, bv2, wo2, bo2, bias_k2, bias_v2, ln_mlp_scale, ln_mlp_offset, w_fc1, b_fc1, w_fc2, b_fc2)
    x = _L0_xattn_ref(x, ctx_2048, mask_BxS2_bf1, L0_xattn_Wq, L0_xattn_Wk, L0_xattn_Wv, L0_xattn_Wo, L0_xattn_ln_gamma, L0_xattn_ln_beta, L0_xattn_gate)
    x = _L1_xattn_ref(x, ctx_2048, ctx_2048, L1_xattn_ln1_scale, L1_xattn_ln1_offset, L1_xattn_wq1, L1_xattn_bq1, L1_xattn_wk1, L1_xattn_bk1, L1_xattn_wv1, L1_xattn_bv1, L1_xattn_wo1, L1_xattn_bo1, L1_xattn_bias_k1, L1_xattn_bias_v1, L1_xattn_ln2_scale, L1_xattn_ln2_offset, L1_xattn_wq2, L1_xattn_bq2, L1_xattn_wk2, L1_xattn_bk2, L1_xattn_wv2, L1_xattn_bv2, L1_xattn_wo2, L1_xattn_bo2, L1_xattn_bias_k2, L1_xattn_bias_v2, L1_xattn_ln_mlp_scale, L1_xattn_ln_mlp_offset, L1_xattn_w_fc1, L1_xattn_b_fc1, L1_xattn_w_fc2, L1_xattn_b_fc2)
    return x

_drawn_inputs = setup_inputs


def setup_inputs(seed=0):
    import zlib

    import numpy as np

    out = dict(_drawn_inputs(seed))
    spreads = {'L0_xattn_ln_gamma': (1.0, 0.6),
     'L0_xattn_ln_beta': (0.0, 0.8),
     'L1_xattn_ln1_scale': (1.0, 0.6),
     'L1_xattn_ln1_offset': (0.0, 0.8),
     'L1_xattn_bq1': (0.0, 0.8),
     'L1_xattn_bk1': (0.0, 2.0),
     'L1_xattn_bv1': (0.0, 0.1),
     'L1_xattn_bo1': (0.0, 0.1),
     'L1_xattn_ln2_scale': (1.0, 0.6),
     'L1_xattn_ln2_offset': (0.0, 0.8),
     'L1_xattn_bq2': (0.0, 0.8),
     'L1_xattn_bk2': (0.0, 2.0),
     'L1_xattn_bv2': (0.0, 0.1),
     'L1_xattn_bo2': (0.0, 0.1),
     'L1_xattn_ln_mlp_scale': (1.0, 0.6),
     'L1_xattn_ln_mlp_offset': (0.0, 0.676),
     'L1_xattn_b_fc1': (0.0, 0.1),
     'L1_xattn_b_fc2': (0.0, 0.1)}
    factors = {'L0_xattn_Wq': 8.0,
     'L0_xattn_Wk': 8.0,
     'L1_xattn_wq1': 8.0,
     'L1_xattn_wk1': 8.0,
     'L1_xattn_bias_k1': 64.0,
     'L1_xattn_bias_v1': 64.0,
     'L1_xattn_wq2': 8.0,
     'L1_xattn_wk2': 8.0,
     'L1_xattn_bias_k2': 64.0,
     'L1_xattn_bias_v2': 64.0}
    for name, (base, spread) in spreads.items():
        noise = np.random.default_rng([zlib.crc32(name.encode()), seed]).standard_normal(out[name].shape)
        drawn = base * np.exp(spread * noise) if base else spread * noise
        out[name] = jnp.asarray(drawn.astype(out[name].dtype))
    for name, factor in factors.items():
        out[name] = (out[name] * factor).astype(out[name].dtype)
    return out
```

```python
from contextlib import ExitStack

import numpy as np
import concourse.bass as bass
from concourse import mybir
from concourse.alu_op_type import AluOpType as ALU

ACT = mybir.ActivationFunctionType
F32 = mybir.dt.float32
F32R = mybir.dt.float32r
U8 = mybir.dt.uint8
AX_X = mybir.AxisListType.X

P = 128
BATCH, SEQ, HID = 4, 256, 256
KT = HID // P
ROWS = BATCH * SEQ
RT = ROWS // P
HEADS = 16
EPS = 1e-5

HD0 = HID // HEADS
HG0 = 4
NG0 = HEADS // HG0
SCALE0 = float(HD0) ** -0.5

LAYERS = 2
HD = 128
GH = 2
GROUPS = HEADS // GH
GW = GH * HD
SCALE = float(HD) ** -0.5
TOK = SEQ + 1
KW = SEQ + 2
BWR = HEADS + 2
STEPS = 16
BODIES = HEADS * BATCH // STEPS
WO_LAG = 6
FF = 1024
FT = FF // P

C_V, C_Q, C_K, C_SMALL, C_O, C_BV, C_END = 0, 512, 1024, 1536, 1542, 2054, 2054 + 2 * GH * BWR
C_LN, C_GATE, C_B1, C_MASK, C_COLS = 0, 16, 17, 25, 29
C0_Q, C0_K, C0_V, C0_O, C0_END = 0, 1024, 2048, 2560, 3584


def first_body(j):
    return isinstance(j, int) and j == 0


def build_program(nc, x_rows, x_t, ctx_rows, ctx_t, mask_rows, cols, ident_in, w0, wg, bo18, w1, w2, b2, out):
    with ExitStack() as ctx:
        def sb(name, shape, dt=F32, on=ctx):
            return on.enter_context(nc.sbuf_tensor(name, shape, dt))

        def sem(name):
            return ctx.enter_context(nc.semaphore(name))

        bank = [ctx.enter_context(nc.psum_tensor(f"bank{i}", [P, 512], F32)) for i in range(8)]

        prm = sb("prm", [P, C_COLS])
        ident = sb("ident", [P, P])
        x = sb("x", [P, RT, HID])
        ctxH, ctxL = sb("ctxH", [P, KT, ROWS], F32R), sb("ctxL", [P, KT, ROWS], F32R)
        hH, hL = sb("hH", [P, KT, ROWS], F32R), sb("hL", [P, KT, ROWS], F32R)
        ln_st = sb("ln_st", [P, RT, 6])
        ln_mv = sb("ln_mv", [P, RT, 2])
        ln_sd = sb("ln_sd", [P, RT])
        ln_rs = sb("ln_rs", [P, RT])
        xn = sb("xn", [P, 4, HID])
        ln_y = sb("ln_y", [P, 2, 512])
        stage = sb("stage", [P, C_END])
        mx = sb("mx", [P, 2, 2])
        nb = sb("nb", [P, 2, 2])
        sm = sb("sm", [P, 2, 2])
        rs = sb("rs", [P, 2, 2])

        l0 = ctx.enter_context(ExitStack())
        anH, anL = sb("anH", [P, KT, ROWS], F32R, l0), sb("anL", [P, KT, ROWS], F32R, l0)
        w0H, w0L = sb("w0H", [P, C0_END], F32R, l0), sb("w0L", [P, C0_END], F32R, l0)
        q0 = sb("q0", [P, NG0, ROWS], F32, l0)
        k0H, k0L = sb("k0H", [P, NG0, ROWS], F32R, l0), sb("k0L", [P, NG0, ROWS], F32R, l0)
        v0 = sb("v0", [P, RT, HID], F32, l0)
        mask8 = sb("mask8", [P, ROWS], U8, l0)
        maskb = sb("maskb", [P, ROWS], F32, l0)
        maskc = sb("maskc", [P, SEQ], F32, l0)
        raws = l0.enter_context(ExitStack())
        w0raw = sb("w0raw", [P, C0_END], F32, raws)
        xt_raw = sb("xt_raw", [P, KT * ROWS], F32, raws)
        ct_raw = sb("ct_raw", [P, KT * ROWS], F32, raws)
        c_rows = sb("c_rows", [P, RT, HID], F32, raws)
        raws.close()
        v0p = sb("v0p", [P, 2, HEADS, P], F32R, l0)
        a0H, a0L = sb("a0H", [P, NG0, SEQ], F32R, l0), sb("a0L", [P, NG0, SEQ], F32R, l0)
        q0m = sb("q0m", [P, 3, SEQ], F32R, l0)
        s0 = sb("s0", [P, 2, 2, SEQ], F32, l0)
        p0 = sb("p0", [P, 2, 2, SEQ], F32, l0)
        pt0H, pt0L = sb("pt0H", [P, 2, 512], F32R, l0), sb("pt0L", [P, 2, 512], F32R, l0)
        l0.close()

        w1raw, w2raw = sb("w1raw", [P, KT * FF]), sb("w2raw", [P, FT * HID])
        w1H, w1L = sb("w1H", [P, KT * FF], F32R), sb("w1L", [P, KT * FF], F32R)
        w2H, w2L = sb("w2H", [P, FT * HID], F32R), sb("w2L", [P, FT * HID], F32R)
        b2b = sb("b2b", [P, HID])
        l1 = ctx.enter_context(ExitStack())
        wH, wL = sb("wH", [P, 2, 2048], F32R, l1), sb("wL", [P, 2, 2048], F32R, l1)
        small = sb("small", [P, 2, 6], F32, l1)
        kbH, kbL = sb("kbH", [P, 2, GH], F32R, l1), sb("kbL", [P, 2, GH], F32R, l1)
        bv = sb("bv", [P, GH * BWR], F32, l1)
        bvH, bvL = sb("bvH", [P, 2, GH * BWR], F32R, l1), sb("bvL", [P, 2, GH * BWR], F32R, l1)
        qH, qL = sb("qH", [P, 2, 512], F32R, l1), sb("qL", [P, 2, 512], F32R, l1)
        kH, kL = sb("kH", [P, 2, 2, KW], F32R, l1), sb("kL", [P, 2, 2, KW], F32R, l1)
        vH, vL = sb("vH", [P, 2, 4, GW], F32R, l1), sb("vL", [P, 2, 4, GW], F32R, l1)
        aH, aL = sb("aH", [P, 2, GH, 512], F32R, l1), sb("aL", [P, 2, GH, 512], F32R, l1)
        pr = sb("pr", [P, 2, 2, TOK], F32, l1)
        ptH, ptL = sb("ptH", [P, 2, 512], F32R, l1), sb("ptL", [P, 2, 512], F32R, l1)
        pb = sb("pb", [P, RT, BWR], F32, l1)
        pbT = sb("pbT", [BWR, ROWS], F32, l1)
        bo = sb("bo", [BWR, LAYERS, HID], F32, l1)
        bw = sb("bw", [BWR, HID], F32, l1)
        l1.close()
        gel = sb("gel", [P, 2, 512])
        gH, gL = sb("gH", [P, FT, ROWS], F32R), sb("gL", [P, FT, ROWS], F32R)
        res = sb("res", [P, RT, HID])

        d_prm, d_ident, d_crows, d_w0, d_xt, d_ct, d_x, d_mask = [
            sem(n) for n in ("d_prm", "d_ident", "d_crows", "d_w0", "d_xt", "d_ct", "d_x", "d_mask")]
        d_wa, d_wo, d_bo, d_w1, d_w2, d_b2, d_out = [
            sem(n) for n in ("d_wa", "d_wo", "d_bo", "d_w1", "d_w2", "d_b2", "d_out")]
        ln_stat, ln_agg, ln_sqrt, ln_rcp, ln_xn, ln_tr, ln_aff, ln_hi, ln_lo = [
            sem(n) for n in ("ln_stat", "ln_agg", "ln_sqrt", "ln_rcp", "ln_xn", "ln_tr", "ln_aff", "ln_hi", "ln_lo")]
        sp_hi, sp_lo, c_hi, c_lo = sem("sp_hi"), sem("sp_lo"), sem("c_hi"), sem("c_lo")
        mask_s, mask_ready, v0p_zero = sem("mask_s"), sem("mask_ready"), sem("v0p_zero")
        gate_t = sem("gate_t")
        pj_mm, pj_hi, pj_lo = sem("pj_mm"), sem("pj_hi"), sem("pj_lo")
        vp_hi, vp_lo, mk_cp = sem("vp_hi"), sem("vp_lo"), sem("mk_cp")
        g_qm, g_s, g_max, g_nb, g_exp, g_rs, g_norm = [
            sem(n) for n in ("g_qm", "g_s", "g_max", "g_nb", "g_exp", "g_rs", "g_norm")]
        g_t, g_pth, g_ptl, g_pv, g_ah, g_al, g_wo, g_add = [
            sem(n) for n in ("g_t", "g_pth", "g_ptl", "g_pv", "g_ah", "g_al", "g_wo", "g_add")]
        w_hi_b = sem("w_hi_b")
        w_hi, w_v, w_q, w_k, w_o, bv_d = sem("w_hi"), sem("w_v"), sem("w_q"), sem("w_k"), sem("w_o"), sem("bv_d")
        kb_cp, pb_ones = sem("kb_cp"), sem("pb_ones")
        s_mm, s_max, s_nb, s_exp, s_rs, s_norm, s_pb = [
            sem(n) for n in ("s_mm", "s_max", "s_nb", "s_exp", "s_rs", "s_norm", "s_pb")]
        t_mm, pt_hi, pt_lo, pv_mm, a_hi, a_lo = [
            sem(n) for n in ("t_mm", "pt_hi", "pt_lo", "pv_mm", "a_hi", "a_lo")]
        v_mm, v_hi, v_lo, o_mm, x_add = [sem(n) for n in ("v_mm", "v_hi", "v_lo", "o_mm", "x_add")]
        q_mm, q_hi, q_lo, k_mm, k_hi, k_lo = [sem(n) for n in ("q_mm", "q_hi", "q_lo", "k_mm", "k_hi", "k_lo")]
        bw_mm, bw_add, pbt_mm, pbt_cp, bx_mm, bx_add = [
            sem(n) for n in ("bw_mm", "bw_add", "pbt_mm", "pbt_cp", "bx_mm", "bx_add")]
        m_whi, m_w, m_xb, f1_mm, f1_gelu, f1_hi, f1_lo, f2_mm, f2_add = [
            sem(n) for n in ("m_whi", "m_w", "m_xb", "f1_mm", "f1_gelu", "f1_hi", "f1_lo", "f2_mm", "f2_add")]

        as_f32 = lambda ap: ap.bitcast(F32)

        def three_passes(pe, dst, lhs, rhs, first, last):
            pe.matmul(dst, lhs[0], rhs[0], start=first, stop=False)
            pe.matmul(dst, lhs[0], rhs[1], start=False, stop=False)
            return pe.matmul(dst, lhs[1], rhs[0], start=False, stop=last)

        SPLITS_A = [("xt", c) for c in range(0, 2048, 512)] + [("w0", c) for c in range(C0_Q, C0_K, 512)]
        SPLITS_B = [("w0", c) for c in range(C0_K, C0_O, 512)]
        N_SPLIT_Q, N_SPLIT_ALL = len(SPLITS_A), len(SPLITS_A) + len(SPLITS_B)

        def split_aps(what, c):
            if what == "xt":
                kt, r = divmod(c, ROWS)
                return xt_raw[:, c:c + 512], hH[:, kt, r:r + 512], hL[:, kt, r:r + 512]
            return w0raw[:, c:c + 512], w0H[:, c:c + 512], w0L[:, c:c + 512]

        def ln_unit(u):
            half, kt = divmod(u, 2)
            return half, kt

        def step(k):
            return (k // 8) % 2, (k // 4) % 2, (k // 2) % 2, k % 2

        block = ctx.enter_context(nc.Block())

        @block.sync
        def _(sp):
            sp.dma_start(c_rows[:, :, :], ctx_rows.rearrange("(r p) c -> p r c", p=P)).then_inc(d_crows, 16)
            sp.dma_start(prm[:, :], cols).then_inc(d_prm, 16)
            sp.dma_start(ident[:, :], ident_in).then_inc(d_ident, 16)
            sp.dma_start(xt_raw[:, :], x_t).then_inc(d_xt, 16)
            sp.dma_start(w0raw[:, :], w0).then_inc(d_w0, 16)
            sp.dma_start(ct_raw[:, :], ctx_t).then_inc(d_ct, 16)
            sp.dma_start(mask8[:, :], mask_rows).then_inc(d_mask, 16)
            sp.dma_start(x[:, :, :], x_rows.rearrange("(r p) c -> p r c", p=P)).then_inc(d_x, 16)
            sp.dma_start(stage[:, 0:C_O], wg[0, :, 0:C_O]).then_inc(d_wa, 16)
            sp.dma_start(stage[:, C_O:C_END], wg[0, :, C_O:C_END]).then_inc(d_wo, 16)
            sp.wait_ge(g_add, 2 * BATCH)
            sp.dma_start(bo[:, :, :], bo18).then_inc(d_bo, 16)
            sp.dma_start(w1raw[:, :], w1).then_inc(d_w1, 16)
            sp.dma_start(w2raw[:, :], w2).then_inc(d_w2, 16)
            sp.dma_start(b2b[:, :], b2).then_inc(d_b2, 16)
            with sp.Fori(1, LAYERS * GROUPS) as n:
                sp.wait_ge(w_k, n)
                sp.dma_start(stage[:, 0:C_O], wg[n, :, 0:C_O]).then_inc(d_wa, 16)
                sp.wait_ge(w_o, n)
                sp.dma_start(stage[:, C_O:C_END], wg[n, :, C_O:C_END]).then_inc(d_wo, 16)
            for r in range(RT):
                sp.wait_ge(f2_add, r + 1)
                sp.dma_start(out[r * P:(r + 1) * P, :], res[:, r, :]).then_inc(d_out, 16)
            sp.wait_ge(d_out, 16 * RT)

        @block.tensor
        def _(pe):
            def ln_transposes(n):
                for u in range(4):
                    half, kt = ln_unit(u)
                    pe.wait_ge(ln_xn, n * RT + 4 * half + 4)
                    if u >= 2:
                        pe.wait_ge(ln_aff, n * 4 + u - 1)
                    for i in range(4):
                        mm = pe.transpose(bank[u % 2][:, i * P:(i + 1) * P], xn[:, i, kt * P:(kt + 1) * P],
                                          ident[:, :])
                    mm.then_inc(ln_tr, 1)

            def proj_bank(i):
                if i >= 6:
                    pe.wait_ge(pj_lo, i - 5)
                return bank[2 + i % 6]

            pe.wait_ge(d_ident, 16)
            ln_transposes(0)
            pe.wait_ge(sp_lo, N_SPLIT_Q)
            for i in range(8):
                g, half = divmod(i, 2)
                dst = proj_bank(i)
                for kt in range(KT):
                    c = C0_Q + kt * 512 + g * P
                    r = slice(half * 512, half * 512 + 512)
                    mm = three_passes(pe, dst[:, :], (w0H[:, c:c + P], w0L[:, c:c + P]),
                                      (hH[:, kt, r], hL[:, kt, r]), kt == 0, kt == KT - 1)
                mm.then_inc(pj_mm, 1)
            pe.wait_ge(sp_lo, N_SPLIT_ALL)
            pe.wait_ge(ln_lo, 4)
            for i in range(8):
                g, half = divmod(i, 2)
                dst = proj_bank(8 + i)
                for kt in range(KT):
                    c = C0_K + kt * 512 + g * P
                    r = slice(half * 512, half * 512 + 512)
                    mm = three_passes(pe, dst[:, :], (w0H[:, c:c + P], w0L[:, c:c + P]),
                                      (anH[:, kt, r], anL[:, kt, r]), kt == 0, kt == KT - 1)
                mm.then_inc(pj_mm, 1)
            for i in range(RT):
                dst = proj_bank(16 + i)
                for kt in range(KT):
                    c = C0_V + kt * HID
                    r = slice(i * P, i * P + P)
                    mm = three_passes(pe, dst[:, 0:HID], (anH[:, kt, r], anL[:, kt, r]),
                                      (w0H[:, c:c + HID], w0L[:, c:c + HID]), kt == 0, kt == KT - 1)
                mm.then_inc(pj_mm, 1)
            pe.wait_ge(c_lo, 6)
            pe.wait_ge(pj_lo, 24)

            with pe.Fori(0, BATCH) as b:
                for k in range(HEADS + 2):
                    if k < HEADS:
                        pe.wait_ge(g_qm, b * HEADS + k + 1)
                        if k >= 2:
                            pe.wait_ge(g_max, b * HEADS + k - 1)
                        for qt in range(2):
                            lhs = q0m[:, k % 3, qt * P:(qt + 1) * P]
                            dst = bank[k % 2][:, qt * SEQ:(qt + 1) * SEQ]
                            pe.matmul(dst, lhs, k0H[:, k // HG0, bass.ds(b * SEQ, SEQ)], start=True, stop=False)
                            mm = pe.matmul(dst, lhs, k0L[:, k // HG0, bass.ds(b * SEQ, SEQ)], start=False, stop=True)
                        mm.then_inc(g_s, 1)
                    if k >= 2:
                        m = k - 2
                        g = m // HG0
                        if m == 0:
                            pe.wait_ge(vp_lo, b + 1)
                        if m % HG0 == 0 and g >= 2:
                            pe.wait_ge(g_al, b * NG0 + g - 1)
                        pe.wait_ge(g_ptl, b * HEADS + m + 1)
                        for tt in range(2):
                            for i, src in enumerate((pt0H, pt0L)):
                                mm = pe.matmul(bank[4 + g % 2][:, 0:SEQ], v0p[:, tt, m, :],
                                               src[:, m % 2, tt * SEQ:(tt + 1) * SEQ],
                                               start=(m % HG0 == 0 and tt == 0 and i == 0),
                                               stop=(m % HG0 == HG0 - 1 and tt == 1 and i == 1))
                        mm.then_inc(g_pv, 1)
                    if 1 <= k <= HEADS:
                        m = k - 1
                        pe.wait_ge(g_norm, b * HEADS + m + 1)
                        if m >= 2:
                            pe.wait_ge(g_ptl, b * HEADS + m - 1)
                        for tt in range(2):
                            for qt in range(2):
                                mm = pe.transpose(bank[2 + m % 2][:, tt * SEQ + qt * P:tt * SEQ + (qt + 1) * P],
                                                  p0[:, m % 2, qt, tt * P:(tt + 1) * P], ident[:, :])
                        mm.then_inc(g_t, 1)
                pe.wait_ge(g_al, b * NG0 + NG0)
                for qt in range(2):
                    for g in range(NG0):
                        q = slice(qt * P, (qt + 1) * P)
                        c = C0_O + g * HID
                        mm = three_passes(pe, bank[6 + qt][:, 0:HID], (a0H[:, g, q], a0L[:, g, q]),
                                          (w0H[:, c:c + HID], w0L[:, c:c + HID]), g == 0, g == NG0 - 1)
                    mm.then_inc(g_wo, 1)

            pe.wait_ge(g_add, 2 * BATCH)

            def weights(part, slot, c, n):
                o = {"v": 0, "q": 512, "k": 1024, "o": 1536}[part] + c
                return wH[:, slot, o:o + n], wL[:, slot, o:o + n]

            def project_v(L, j, m):
                slot, bp = (m // 8) % 2, (m // 4) % 2
                if m % 8 == 0:
                    pe.wait_ge(w_v, L * GROUPS + j * 2 + m // 8 + 1)
                if not (first_body(j) and m == 0):
                    pe.wait_ge(v_lo, L * 64 + j * STEPS + m)
                r = slice((bp * 4 + m % 4) * P, (bp * 4 + m % 4 + 1) * P)
                for kt in range(KT):
                    mm = three_passes(pe, bank[6][:, 0:GW], (ctxH[:, kt, r], ctxL[:, kt, r]),
                                      weights("v", slot, kt * GW, GW), kt == 0, kt == KT - 1)
                mm.then_inc(v_mm, 1)

            def project_qk(L, j, u, is_q):
                slot, bp, h = (u // 4) % 2, (u // 2) % 2, u % 2
                ready, free, done, to = (w_q, q_lo, q_mm, 4) if is_q else (w_k, k_lo, k_mm, 5)
                if u % 4 == 0:
                    pe.wait_ge(ready, L * GROUPS + j * 2 + u // 4 + 1)
                if not (first_body(j) and u == 0):
                    pe.wait_ge(free, L * 32 + j * 8 + u)
                inH, inL = (hH, hL) if is_q else (ctxH, ctxL)
                r = slice(bp * 512, bp * 512 + 512)
                for kt in range(KT):
                    mm = three_passes(pe, bank[to][:, :], weights("q" if is_q else "k", slot, kt * GW + h * HD, HD),
                                      (inH[:, kt, r], inL[:, kt, r]), kt == 0, kt == KT - 1)
                mm.then_inc(done, 1)

            def scores(L, j, k):
                slot = (k // 2) % 2
                if k % 2 == 0:
                    pe.wait_ge(q_lo, L * 32 + j * 8 + k // 2 + 1)
                    pe.wait_ge(k_lo, L * 32 + j * 8 + k // 2 + 1)
                    pe.wait_ge(kb_cp, L * 32 + j * 8 + k // 2 + 1)
                if not (first_body(j) and k == 0):
                    pe.wait_ge(s_exp, L * 64 + j * STEPS + k)
                b = k % 2
                for qt in range(2):
                    q = slice(b * SEQ + qt * P, b * SEQ + (qt + 1) * P)
                    mm = three_passes(pe, bank[qt][:, 0:KW], (qH[:, slot, q], qL[:, slot, q]),
                                      (kH[:, slot, b, :], kL[:, slot, b, :]), True, True)
                mm.then_inc(s_mm, 1)

            def values(L, j, k):
                slot, bp, h, b = step(k)
                vs = (k // 4) % 2
                pe.wait_ge(pt_lo, L * 64 + j * STEPS + k + 1)
                pe.wait_ge(v_lo, L * 64 + j * STEPS + k // 4 * 4 + b * 2 + 2)
                if not (first_body(j) and k == 0):
                    pe.wait_ge(a_lo, L * 64 + j * STEPS + k)
                for tt in range(2):
                    d = slice(h * HD, (h + 1) * HD)
                    t = slice(tt * SEQ, (tt + 1) * SEQ)
                    mm = three_passes(pe, bank[3][:, 0:SEQ], (vH[:, vs, b * 2 + tt, d], vL[:, vs, b * 2 + tt, d]),
                                      (ptH[:, k % 2, t], ptL[:, k % 2, t]), tt == 0, tt == 1)
                mm.then_inc(pv_mm, 1)

            def transposes(L, j, k):
                pe.wait_ge(s_norm, L * 64 + j * STEPS + k + 1)
                if not (first_body(j) and k == 0):
                    pe.wait_ge(pt_lo, L * 64 + j * STEPS + k)
                for tt in range(2):
                    for qt in range(2):
                        mm = pe.transpose(bank[2][:, tt * SEQ + qt * P:tt * SEQ + (qt + 1) * P],
                                          pr[:, k % 2, qt, tt * P:(tt + 1) * P], ident[:, :])
                mm.then_inc(t_mm, 1)

            def output(L, j, m):
                slot, vs, i = (m // 8) % 2, (m // 4) % 2, m % 4
                b = i // 2
                if m % 8 == 0:
                    pe.wait_ge(w_o, L * GROUPS + j * 2 + m // 8 + 1)
                pe.wait_ge(a_lo, L * 64 + j * STEPS + m // 4 * 4 + 3 + b)
                if not (first_body(j) and m == 0):
                    pe.wait_ge(x_add, L * 64 + j * STEPS + m)
                if m % 8 == 2:
                    pe.wait_ge(bw_add, L * GROUPS + j * 2 + (m + WO_LAG) // 8)
                for h in range(GH):
                    q = slice(i * P, (i + 1) * P)
                    mm = three_passes(pe, bank[7][:, 0:HID], (aH[:, vs, h, q], aL[:, vs, h, q]),
                                      weights("o", slot, h * HID, HID), h == 0, h == GH - 1)
                mm.then_inc(o_mm, 1)

            def bias_product(L, j, g):
                if g == 0:
                    pe.wait_ge(x_add, L * 64 + j * STEPS + 7 - WO_LAG + 1)
                else:
                    pe.wait_ge(x_add, L * 64 + j * STEPS + 15 - WO_LAG + 1)
                pe.wait_ge(w_o, L * GROUPS + j * 2 + g + 1)
                for h in range(GH):
                    c = slice(h * BWR, (h + 1) * BWR)
                    mm = three_passes(pe, bank[7][0:BWR, 0:HID], (bvH[:, g, c], bvL[:, g, c]),
                                      weights("o", g, h * HID, HID), h == 0, h == GH - 1)
                mm.then_inc(bw_mm, 1)

            def body(L, j, first=False, last=False):
                for k in range(STEPS + (WO_LAG if last else 0)):
                    if k < STEPS:
                        scores(L, j, k)
                    if (k >= 2 or not first) and k - 2 < STEPS:
                        values(L, j, k - 2)
                    if (k >= 1 or not first) and k - 1 < STEPS:
                        transposes(L, j, k - 1)
                    if k < STEPS and not (last and k + 4 >= STEPS):
                        project_v(L, j, k + 4)
                    if k >= WO_LAG or not first:
                        output(L, j, k - WO_LAG)
                    if k < STEPS and not (last and k // 2 + 1 >= STEPS // 2):
                        project_qk(L, j, k // 2 + 1, k % 2 == 0)
                    if k < STEPS and k % 8 == 7:
                        bias_product(L, j, k // 8)

            with pe.Fori(0, LAYERS) as L:
                if True:
                    pe.wait_ge(c_lo, 6)
                    for i in range(4):
                        project_v(L, 0, i)
                    project_qk(L, 0, 0, False)
                    ln_transposes(L + 1)
                    pe.wait_ge(ln_lo, (L + 1) * 4 + 4)
                    project_qk(L, 0, 0, True)
                body(L, 0, first=True)
                with pe.Fori(1, BODIES - 1) as j:
                    body(L, j)
                body(L, BODIES - 1, last=True)
                pe.wait_ge(s_pb, L * 64 + 64)
                for r in range(RT):
                    mm = pe.transpose(bank[4 + r // 4][0:BWR, (r % 4) * P:(r % 4 + 1) * P], pb[:, r, :], ident[:, :])
                    if r % 4 == 3:
                        mm.then_inc(pbt_mm, 1)
                pe.wait_ge(bw_add, L * GROUPS + GROUPS)
                for r in range(RT):
                    pe.wait_ge(pbt_cp, L * 2 + r // 4 + 1)
                    if r >= 2:
                        pe.wait_ge(bx_add, L * RT + r - 1)
                    pe.matmul(bank[r % 2][:, 0:HID], pbT[:, r * P:(r + 1) * P], bw[:, :],
                              start=True, stop=True).then_inc(bx_mm, 1)

            ln_transposes(LAYERS + 1)
            pe.wait_ge(ln_lo, (LAYERS + 1) * 4 + 4)
            pe.wait_ge(m_w, 4)
            for i in range(2 * FT):
                half, f = divmod(i, FT)
                if i >= 2:
                    pe.wait_ge(f1_gelu, i - 1)
                for kt in range(KT):
                    c = slice(kt * FF + f * P, kt * FF + (f + 1) * P)
                    r = slice(half * 512, half * 512 + 512)
                    mm = three_passes(pe, bank[2 + i % 2][:, :], (w1H[:, c], w1L[:, c]),
                                      (hH[:, kt, r], hL[:, kt, r]), kt == 0, kt == KT - 1)
                mm.then_inc(f1_mm, 1)
            pe.wait_ge(m_w, 8)
            for r in range(RT):
                pe.wait_ge(f1_lo, (r // 4 + 1) * FT)
                if r >= 2:
                    pe.wait_ge(f2_add, r - 1)
                for f in range(FT):
                    q = slice(r * P, (r + 1) * P)
                    c = slice(f * HID, (f + 1) * HID)
                    mm = three_passes(pe, bank[4 + r % 2][:, 0:HID], (gH[:, f, q], gL[:, f, q]),
                                      (w2H[:, c], w2L[:, c]), f == 0, f == FT - 1)
                mm.then_inc(f2_mm, 1)

        @block.scalar
        def _(act):
            def ln_sqrts(n):
                act.wait_ge(ln_agg, n * 2 + 2)
                act.activation(ln_sd[:, :], ln_sd[:, :], ACT.Sqrt).then_inc(ln_sqrt, 1)

            def ln_his(n):
                for u in range(4):
                    half, kt = ln_unit(u)
                    act.wait_ge(ln_aff, n * 4 + u + 1)
                    dst = (anH if first_body(n) else hH)[:, kt, half * 512:half * 512 + 512]
                    act.activation(dst, ln_y[:, u % 2, :], ACT.Copy).then_inc(ln_hi, 1)

            def split_his(parts):
                for what, c in parts:
                    src, hi, _ = split_aps(what, c)
                    act.activation(hi, src, ACT.Copy).then_inc(sp_hi, 1)

            act.wait_ge(d_prm, 16)
            act.activation(prm[:, C_GATE:C_GATE + 1], prm[:, C_GATE:C_GATE + 1], ACT.Tanh).then_inc(gate_t, 1)
            ln_sqrts(0)
            act.wait_ge(d_xt, 16)
            act.wait_ge(d_w0, 16)
            split_his(SPLITS_A)
            ln_his(0)
            split_his(SPLITS_B)
            for i in range(24):
                act.wait_ge(pj_mm, i + 1)
                src = bank[2 + i % 6]
                if i < 16:
                    g, half = divmod(i % 8, 2)
                    dst = (q0 if i < 8 else k0H)[:, g, half * 512:half * 512 + 512]
                    if i < 8:
                        act.activation(dst.bitcast(F32R), src[:, :], ACT.Copy).then_inc(pj_hi, 1)
                    else:
                        act.activation(dst, src[:, :], ACT.Copy).then_inc(pj_hi, 1)
            act.wait_ge(v0p_zero, 1)
            act.wait_ge(pj_lo, 24)
            with act.Fori(0, BATCH) as b:
                for tt in range(2):
                    dst = v0p[:, tt, :, :].rearrange("p (g j) c -> p g (j c)", g=NG0)
                    for j in range(HG0):
                        hi = act.activation(dst[:, :, j * 160:j * 160 + HD0],
                                            v0[:, b * 2 + tt, :].rearrange("p (g j d) -> p g j d", g=NG0, j=HG0)[:, :, j, :],
                                            ACT.Copy)
                hi.then_inc(vp_hi, 1)
                for k in range(HEADS + 2):
                    if k < HEADS:
                        act.wait_ge(g_nb, b * HEADS + k + 1)
                        if k >= 2:
                            act.wait_ge(g_t, b * HEADS + k - 1)
                        for qt in range(2):
                            e = act.activation(p0[:, k % 2, qt, :], s0[:, k % 2, qt, :], ACT.Exp,
                                               bias=nb[:, k % 2, qt:qt + 1], scale=SCALE0,
                                               accum_out=sm[:, k % 2, qt:qt + 1])
                        e.then_inc(g_exp, 1)
                    if k >= 2 and (k - 2) % HG0 == HG0 - 1:
                        g = (k - 2) // HG0
                        act.wait_ge(g_pv, b * HEADS + k - 1)
                        act.activation(a0H[:, g, :], bank[4 + g % 2][:, 0:SEQ], ACT.Copy).then_inc(g_ah, 1)
                    if 1 <= k <= HEADS:
                        m = k - 1
                        act.wait_ge(g_t, b * HEADS + m + 1)
                        if m >= 2:
                            act.wait_ge(g_pv, b * HEADS + m - 1)
                        act.activation(pt0H[:, m % 2, :], bank[2 + m % 2][:, :], ACT.Copy).then_inc(g_pth, 1)

            def body(L, j, first=False, last=False):
                for k in range(STEPS + (WO_LAG if last else 0)):
                    if k < STEPS:
                        act.wait_ge(s_nb, L * 64 + j * STEPS + k + 1)
                        if not (first_body(j) and k < 2):
                            act.wait_ge(t_mm, L * 64 + j * STEPS + k - 1)
                            act.wait_ge(s_pb, L * 64 + j * STEPS + k - 1)
                        for qt in range(2):
                            e = act.activation(pr[:, k % 2, qt, :], bank[qt][:, 0:TOK], ACT.Exp,
                                               bias=nb[:, k % 2, qt:qt + 1], scale=SCALE,
                                               accum_out=sm[:, k % 2, qt:qt + 1])
                        e.then_inc(s_exp, 1)
                    if (k >= 2 or not first) and k - 2 < STEPS:
                        m = k - 2
                        _, _, h, b = step(m)
                        act.wait_ge(pv_mm, L * 64 + j * STEPS + m + 1)
                        act.activation(aH[:, (m // 4) % 2, h, b * SEQ:(b + 1) * SEQ], bank[3][:, 0:SEQ],
                                       ACT.Copy).then_inc(a_hi, 1)
                    if (k >= 1 or not first) and k - 1 < STEPS:
                        m = k - 1
                        act.wait_ge(t_mm, L * 64 + j * STEPS + m + 1)
                        act.activation(ptH[:, m % 2, :], bank[2][:, :], ACT.Copy).then_inc(pt_hi, 1)
                    if k < STEPS and not (last and k + 4 >= STEPS):
                        project_v_hi(L, j, k + 4)
                    if k < STEPS and not (last and k // 2 + 1 >= STEPS // 2):
                        project_qk_hi(L, j, k // 2 + 1, k % 2 == 0)

            def project_v_hi(L, j, m):
                act.wait_ge(v_mm, L * 64 + j * STEPS + m + 1)
                act.activation(vH[:, (m // 4) % 2, m % 4, :], bank[6][:, 0:GW], ACT.Copy).then_inc(v_hi, 1)

            def project_qk_hi(L, j, u, is_q):
                g, h = (u // 4) % 2, u % 2
                if is_q:
                    act.wait_ge(q_mm, L * 32 + j * 8 + u + 1)
                    act.activation(qH[:, u % 2, :], bank[4][:, :], ACT.Identity,
                                   bias=small[:, g, h:h + 1]).then_inc(q_hi, 1)
                else:
                    act.wait_ge(k_mm, L * 32 + j * 8 + u + 1)
                    act.activation(kH[:, u % 2, :, 0:SEQ], bank[5][:, :].rearrange("p (b t) -> p b t", b=2),
                                   ACT.Identity, bias=small[:, g, 2 + h:3 + h]).then_inc(k_hi, 1)

            with act.Fori(0, LAYERS) as L:
                for i in range(4):
                    project_v_hi(L, 0, i)
                project_qk_hi(L, 0, 0, False)
                ln_sqrts(L + 1)
                ln_his(L + 1)
                project_qk_hi(L, 0, 0, True)
                body(L, 0, first=True)
                with act.Fori(1, BODIES - 1) as j:
                    body(L, j)
                body(L, BODIES - 1, last=True)
                for i in range(2):
                    act.wait_ge(pbt_mm, L * 2 + i + 1)
                    act.activation(pbT[:, i * 512:(i + 1) * 512], bank[4 + i][0:BWR, :], ACT.Copy).then_inc(pbt_cp, 1)

            ln_sqrts(LAYERS + 1)
            ln_his(LAYERS + 1)
            for i in range(2 * FT):
                f = i % FT
                act.wait_ge(f1_mm, i + 1)
                if i >= 2:
                    act.wait_ge(f1_lo, i - 1)
                act.activation(gel[:, i % 2, :], bank[2 + i % 2][:, :], ACT.Gelu,
                               bias=prm[:, C_B1 + f:C_B1 + f + 1]).then_inc(f1_gelu, 1)

        @block.vector
        def _(dve):
            def ln_rows(n, src):
                for r in range(RT):
                    st = dve.bn_stats(ln_st[:, r, :], src[:, r, :])
                st.then_inc(ln_stat, 1)
                dve.wait_ge(ln_stat, n + 1)
                dve.nop(nofuse=True)
                for r in range(RT):
                    ag = dve.bn_aggr(ln_mv[:, r, :], ln_st[:, r, :])
                ag.then_inc(ln_agg, 1)
                dve.wait_ge(ln_agg, n * 2 + 1)
                dve.tensor_scalar(ln_sd[:, :], ln_mv[:, :, 1], EPS, None, ALU.add).then_inc(ln_agg, 1)
                dve.wait_ge(ln_sqrt, n + 1)
                dve.reciprocal(ln_rs[:, :], ln_sd[:, :]).then_inc(ln_rcp, 1)
                dve.wait_ge(ln_rcp, n + 1)
                for r in range(RT):
                    if r == 4:
                        dve.wait_ge(ln_tr, n * 4 + 2)
                    dve.tensor_scalar(xn[:, r % 4, :], src[:, r, :], ln_mv[:, r, 0:1], ln_rs[:, r:r + 1],
                                      ALU.subtract, ALU.mult).then_inc(ln_xn, 1)

            def ln_affine(n):
                H, Lo = (anH, anL) if first_body(n) else (hH, hL)
                for u in range(5):
                    if u < 4:
                        half, kt = ln_unit(u)
                        dve.wait_ge(ln_tr, n * 4 + u + 1)
                        if u >= 2:
                            dve.wait_ge(ln_lo, n * 4 + u - 1)
                        c = C_LN + n * 4 + kt
                        dve.tensor_scalar(ln_y[:, u % 2, :], bank[u % 2][:, :], prm[:, bass.ds(c, 1)],
                                          prm[:, bass.ds(c + 2, 1)], ALU.mult, ALU.add).then_inc(ln_aff, 1)
                    if u >= 1:
                        half, kt = ln_unit(u - 1)
                        dve.wait_ge(ln_hi, n * 4 + u)
                        r = slice(half * 512, half * 512 + 512)
                        dve.tensor_tensor(Lo[:, kt, r], ln_y[:, (u - 1) % 2, :], as_f32(H[:, kt, r]),
                                          ALU.subtract).then_inc(ln_lo, 1)

            def split_los(parts, n0):
                for n, (what, c) in enumerate(parts):
                    src, hi, lo = split_aps(what, c)
                    dve.wait_ge(sp_hi, n0 + n + 1)
                    dve.tensor_tensor(lo, src, as_f32(hi), ALU.subtract).then_inc(sp_lo, 1)

            dve.wait_ge(d_prm, 16)
            dve.wait_ge(d_crows, 16)
            ln_rows(0, c_rows)
            split_los(SPLITS_A, 0)
            ln_affine(0)
            split_los(SPLITS_B, N_SPLIT_Q)
            for i in range(24):
                src = bank[2 + i % 6]
                if i < 16:
                    g, half = divmod(i % 8, 2)
                    r = slice(half * 512, half * 512 + 512)
                    dve.wait_ge(pj_hi, i + 1)
                    if i < 8:
                        dve.tensor_tensor(q0[64:P, g, r], src[64:P, :], q0[64:P, g, r],
                                          ALU.subtract).then_inc(pj_lo, 1)
                    else:
                        dve.tensor_tensor(k0L[:, g, r], src[:, :], as_f32(k0H[:, g, r]),
                                          ALU.subtract).then_inc(pj_lo, 1)
                else:
                    dve.wait_ge(pj_mm, i + 1)
                    dve.tensor_copy(v0[:, i - 16, :], src[:, 0:HID]).then_inc(pj_lo, 1)
            dve.wait_ge(d_mask, 16)
            dve.tensor_copy(maskb[:, :], mask8[:, :]).then_inc(mask_s, 1)
            dve.wait_ge(mask_s, 1)
            dve.reciprocal(maskb[:, :], maskb[:, :]).then_inc(mask_s, 1)
            dve.wait_ge(mask_s, 2)
            dve.tensor_scalar(maskb[:, :], maskb[:, :], -1.0, 1.0, ALU.mult, ALU.add).then_inc(mask_ready, 1)
            dve.wait_ge(mask_ready, 1)
            dve.wait_ge(d_x, 16)
            dve.wait_ge(gate_t, 1)
            dve.wait_ge(pj_lo, 24)
            with dve.Fori(0, BATCH) as b:
                dve.tensor_copy(maskc[:, :], maskb[:, bass.ds(b * SEQ, SEQ)]).then_inc(mk_cp, 1)
                dve.wait_ge(vp_hi, b + 1)
                for tt in range(2):
                    dst = v0p[:, tt, :, :].rearrange("p (g j) c -> p g (j c)", g=NG0)
                    for j in range(HG0):
                        lo = dve.tensor_tensor(
                            dst[:, :, j * 160 + HD0:j * 160 + 2 * HD0],
                            v0[:, b * 2 + tt, :].rearrange("p (g j d) -> p g j d", g=NG0, j=HG0)[:, :, j, :],
                            as_f32(dst[:, :, j * 160:j * 160 + HD0]), ALU.subtract)
                lo.then_inc(vp_lo, 1)
                dve.wait_ge(mk_cp, b + 1)
                for k in range(HEADS + 2):
                    if k < HEADS:
                        dve.wait_ge(g_s, b * HEADS + k + 1)
                        if k >= 2:
                            dve.wait_ge(g_exp, b * HEADS + k - 1)
                        dve.nop(nofuse=True)
                        for qt in range(2):
                            t = dve.tensor_tensor_reduce(
                                out=s0[:, k % 2, qt, :], in0=bank[k % 2][:, qt * SEQ:(qt + 1) * SEQ],
                                in1=maskc[:, :], scale=1.0, scalar=-3.0e38, op0=ALU.add, op1=ALU.max,
                                accum_out=mx[:, k % 2, qt:qt + 1])
                        t.then_inc(g_max, 1)
                        dve.wait_ge(g_max, b * HEADS + k + 1)
                        dve.tensor_scalar(nb[:, k % 2, :], mx[:, k % 2, :], -SCALE0, None,
                                          ALU.mult).then_inc(g_nb, 1)
                    if k >= 2 and (k - 2) % HG0 == HG0 - 1:
                        g = (k - 2) // HG0
                        dve.wait_ge(g_ah, b * NG0 + g + 1)
                        dve.tensor_tensor(a0L[:, g, :], bank[4 + g % 2][:, 0:SEQ], as_f32(a0H[:, g, :]),
                                          ALU.subtract).then_inc(g_al, 1)
                    if k < HEADS:
                        dve.wait_ge(g_exp, b * HEADS + k + 1)
                        dve.reciprocal(rs[:, k % 2, :], sm[:, k % 2, :]).then_inc(g_rs, 1)
                    if 1 <= k <= HEADS:
                        m = k - 1
                        dve.wait_ge(g_pth, b * HEADS + m + 1)
                        dve.tensor_tensor(pt0L[:, m % 2, :], bank[2 + m % 2][:, :], as_f32(pt0H[:, m % 2, :]),
                                          ALU.subtract).then_inc(g_ptl, 1)
                for qt in range(2):
                    dve.wait_ge(g_wo, b * 2 + qt + 1)
                    dve.scalar_tensor_tensor(x[:, b * 2 + qt, :], bank[6 + qt][:, 0:HID], prm[:, C_GATE:C_GATE + 1],
                                             x[:, b * 2 + qt, :], ALU.mult, ALU.add).then_inc(g_add, 1)
            dve.wait_ge(g_add, 2 * BATCH)

            def project_v_lo(L, j, m):
                dve.wait_ge(v_hi, L * 64 + j * STEPS + m + 1)
                s = (m // 4) % 2
                dve.tensor_tensor(vL[:, s, m % 4, :], bank[6][:, 0:GW], as_f32(vH[:, s, m % 4, :]),
                                  ALU.subtract).then_inc(v_lo, 1)

            def project_qk_lo(L, j, u, is_q):
                g, h = (u // 4) % 2, u % 2
                if is_q:
                    dve.wait_ge(q_hi, L * 32 + j * 8 + u + 1)
                    dve.scalar_tensor_tensor(qL[:, u % 2, :], bank[4][:, :], small[:, g, h:h + 1],
                                             as_f32(qH[:, u % 2, :]), ALU.add, ALU.subtract).then_inc(q_lo, 1)
                else:
                    dve.wait_ge(k_hi, L * 32 + j * 8 + u + 1)
                    dve.scalar_tensor_tensor(kL[:, u % 2, :, 0:SEQ], bank[5][:, :].rearrange("p (b t) -> p b t", b=2),
                                             small[:, g, 2 + h:3 + h], as_f32(kH[:, u % 2, :, 0:SEQ]),
                                             ALU.add, ALU.subtract).then_inc(k_lo, 1)

            def body(L, j, first=False, last=False):
                for k in range(STEPS + (WO_LAG if last else 0)):
                    if k < STEPS:
                        dve.wait_ge(s_mm, L * 64 + j * STEPS + k + 1)
                        for qt in range(2):
                            t = dve.tensor_reduce(mx[:, k % 2, qt:qt + 1], bank[qt][:, 0:TOK], AX_X, ALU.max)
                        t.then_inc(s_max, 1)
                        dve.wait_ge(s_max, L * 64 + j * STEPS + k + 1)
                        dve.tensor_scalar(nb[:, k % 2, :], mx[:, k % 2, :], -SCALE, None,
                                          ALU.mult).then_inc(s_nb, 1)
                    if (k >= 2 or not first) and k - 2 < STEPS:
                        m = k - 2
                        _, _, h, b = step(m)
                        dve.wait_ge(a_hi, L * 64 + j * STEPS + m + 1)
                        t = slice(b * SEQ, (b + 1) * SEQ)
                        dve.tensor_tensor(aL[:, (m // 4) % 2, h, t], bank[3][:, 0:SEQ],
                                          as_f32(aH[:, (m // 4) % 2, h, t]), ALU.subtract).then_inc(a_lo, 1)
                    if k < STEPS:
                        dve.wait_ge(s_exp, L * 64 + j * STEPS + k + 1)
                        dve.reciprocal(rs[:, k % 2, :], sm[:, k % 2, :]).then_inc(s_rs, 1)
                    if (k >= 1 or not first) and k - 1 < STEPS:
                        m = k - 1
                        dve.wait_ge(pt_hi, L * 64 + j * STEPS + m + 1)
                        dve.tensor_tensor(ptL[:, m % 2, :], bank[2][:, :], as_f32(ptH[:, m % 2, :]),
                                          ALU.subtract).then_inc(pt_lo, 1)
                    if k < STEPS and not (last and k + 4 >= STEPS):
                        project_v_lo(L, j, k + 4)
                    if k >= WO_LAG or not first:
                        m = k - WO_LAG
                        rt = (m // 4) % 2 * 4 + m % 4
                        dve.wait_ge(o_mm, L * 64 + j * STEPS + m + 1)
                        dve.tensor_tensor(x[:, rt, :], bank[7][:, 0:HID], x[:, rt, :], ALU.add).then_inc(x_add, 1)
                    if k < STEPS and not (last and k // 2 + 1 >= STEPS // 2):
                        project_qk_lo(L, j, k // 2 + 1, k % 2 == 0)
                    if k < STEPS and k % 8 == 7:
                        dve.wait_ge(bw_mm, L * GROUPS + j * 2 + k // 8 + 1)
                        other = bo[:, L, :] if first and k < 8 else bw[:, :]
                        dve.tensor_tensor(bw[:, :], bank[7][0:BWR, 0:HID], other, ALU.add).then_inc(bw_add, 1)

            dve.wait_ge(d_bo, 16)
            with dve.Fori(0, LAYERS) as L:
                for i in range(4):
                    project_v_lo(L, 0, i)
                project_qk_lo(L, 0, 0, False)
                ln_rows(L + 1, x)
                ln_affine(L + 1)
                project_qk_lo(L, 0, 0, True)
                body(L, 0, first=True)
                with dve.Fori(1, BODIES - 1) as j:
                    body(L, j)
                body(L, BODIES - 1, last=True)
                for r in range(RT):
                    dve.wait_ge(bx_mm, L * RT + r + 1)
                    dve.tensor_tensor(x[:, r, :], bank[r % 2][:, 0:HID], x[:, r, :], ALU.add).then_inc(bx_add, 1)
                dve.wait_ge(bx_add, L * RT + RT)

            ln_rows(LAYERS + 1, x)
            ln_affine(LAYERS + 1)
            dve.wait_ge(d_b2, 16)
            for r in range(RT):
                t = dve.tensor_tensor(x[:, r, :], x[:, r, :], b2b[:, :], ALU.add)
            t.then_inc(m_xb, 1)
            for i in range(2 * FT):
                half, f = divmod(i, FT)
                r = slice(half * 512, half * 512 + 512)
                dve.wait_ge(f1_gelu, i + 1)
                dve.tensor_copy(gH[:, f, r], gel[:, i % 2, :]).then_inc(f1_hi, 1)
                dve.wait_ge(f1_hi, i + 1)
                dve.tensor_tensor(gL[:, f, r], gel[:, i % 2, :], as_f32(gH[:, f, r]), ALU.subtract).then_inc(f1_lo, 1)
            dve.wait_ge(m_xb, 1)
            for r in range(RT):
                dve.wait_ge(f2_mm, r + 1)
                dve.tensor_tensor(res[:, r, :], bank[4 + r % 2][:, 0:HID], x[:, r, :], ALU.add).then_inc(f2_add, 1)

        @block.gpsimd
        def _(pool):
            def split(src, hi, lo, count, hi_sem, lo_sem):
                pool.tensor_scalar(hi, src, 1.0, 1.0, ALU.mult, ALU.mult).then_inc(hi_sem, 1)
                pool.wait_ge(hi_sem, count)
                pool.nop(nofuse=True)
                return pool.tensor_tensor(lo, src, as_f32(hi), ALU.subtract).then_inc(lo_sem, 1)

            pool.wait_ge(d_ct, 16)
            pool.nop(nofuse=True)
            for i in range(4):
                kt, r = divmod(i * 512, ROWS)
                split(ct_raw[:, i * 512:(i + 1) * 512], ctxH[:, kt, r:r + 512], ctxL[:, kt, r:r + 512],
                      i + 1, c_hi, c_lo)
            pool.wait_ge(d_w0, 16)
            pool.nop(nofuse=True)
            for i in range(2):
                c = slice(C0_O + i * 512, C0_O + (i + 1) * 512)
                split(w0raw[:, c], w0H[:, c], w0L[:, c], 5 + i, c_hi, c_lo)
            pool.wait_ge(sp_lo, N_SPLIT_ALL)
            pool.wait_ge(ln_xn, RT)
            pool.wait_ge(c_lo, 6)
            pool.nop(nofuse=True)
            pool.memset(as_f32(v0p[:, :, :, :]), 0.0).then_inc(v0p_zero, 1)
            pool.wait_ge(pj_lo, 24)
            pool.nop(nofuse=True)

            def masked_q(b, k):
                pool.tensor_tensor(q0m[:, k % 3, :], q0[:, k // HG0, bass.ds(b * SEQ, SEQ)],
                                   prm[:, C_MASK + k % HG0:C_MASK + k % HG0 + 1].to_broadcast([P, SEQ]),
                                   ALU.mult).then_inc(g_qm, 1)

            with pool.Fori(0, BATCH) as b:
                masked_q(b, 0)
                masked_q(b, 1)
                for k in range(HEADS):
                    if k + 2 < HEADS:
                        if k >= 1:
                            pool.wait_ge(g_s, b * HEADS + k)
                        pool.nop(nofuse=True)
                        masked_q(b, k + 2)
                    pool.wait_ge(g_rs, b * HEADS + k + 1)
                    pool.nop(nofuse=True)
                    for qt in range(2):
                        t = pool.tensor_scalar(p0[:, k % 2, qt, :], p0[:, k % 2, qt, :], rs[:, k % 2, qt:qt + 1], 1.0,
                                               ALU.mult, ALU.mult)
                    t.then_inc(g_norm, 1)

            pool.wait_ge(g_add, 2 * BATCH)
            pool.nop(nofuse=True)
            pool.memset(pb[:, :, HEADS:BWR], 1.0).then_inc(pb_ones, 1)

            def split_v(n, g):
                pool.wait_ge(d_wa, n * 16 + 16)
                pool.nop(nofuse=True)
                pool.tensor_copy(small[:, g, :], stage[:, C_SMALL:C_O])
                split(stage[:, C_SMALL + 4:C_O], kbH[:, g, :], kbL[:, g, :], n * 6 + 1, w_hi, w_hi_b)
                split(stage[:, C_V:C_Q], wH[:, g, 0:512], wL[:, g, 0:512], n * 6 + 2, w_hi, w_v)

            def split_q(n, g):
                split(stage[:, C_Q:C_K], wH[:, g, 512:1024], wL[:, g, 512:1024], n * 6 + 3, w_hi, w_q)

            def split_k(n, g):
                split(stage[:, C_K:C_SMALL], wH[:, g, 1024:1536], wL[:, g, 1024:1536], n * 6 + 4, w_hi, w_k)

            def split_o(n, g):
                pool.wait_ge(d_wo, n * 16 + 16)
                pool.nop(nofuse=True)
                pool.tensor_tensor(bv[:, :], stage[:, C_BV:C_BV + GH * BWR], stage[:, C_BV + GH * BWR:C_END],
                                   ALU.subtract).then_inc(bv_d, 1)
                pool.wait_ge(bv_d, n + 1)
                pool.nop(nofuse=True)
                split(bv[:, :], bvH[:, g, :], bvL[:, g, :], n * 6 + 5, w_hi, w_hi_b)
                split(stage[:, C_O:C_BV], wH[:, g, 1536:2048], wL[:, g, 1536:2048], n * 6 + 6, w_hi, w_o)

            def key_bias(L, j, u):
                g, h = (u // 4) % 2, u % 2
                pool.wait_ge(w_hi_b, L * GROUPS * 2 + j * 4 + (u // 4) * 2 + 1)
                pool.nop(nofuse=True)
                if not (first_body(j) and u < 2):
                    pool.wait_ge(s_mm, L * 64 + j * STEPS + 2 * (u - 1))
                pool.nop(nofuse=True)
                for dst, src in ((kH, kbH), (kL, kbL)):
                    t = pool.tensor_copy(dst[:, u % 2, :, SEQ:KW], as_r(src, g, h))
                t.then_inc(kb_cp, 1)

            def as_r(src, g, h):
                return src[:, g, h:h + 1].unsqueeze(2).to_broadcast([P, 2, 2])

            def body(L, j, first=False, last=False):
                for k in range(STEPS):
                    if k % 2 == 0 and not (last and k // 2 + 1 >= STEPS // 2):
                        key_bias(L, j, k // 2 + 1)
                    slot, bp, h, b = step(k)
                    pool.wait_ge(s_rs, L * 64 + j * STEPS + k + 1)
                    pool.nop(nofuse=True)
                    for qt in range(2):
                        t = pool.tensor_scalar(pr[:, k % 2, qt, :], pr[:, k % 2, qt, :], rs[:, k % 2, qt:qt + 1], 1.0,
                                               ALU.mult, ALU.mult)
                    t.then_inc(s_norm, 1)
                    pool.wait_ge(s_norm, L * 64 + j * STEPS + k + 1)
                    pool.nop(nofuse=True)
                    rt = (bp * 2 + b) * 2
                    head = j * 4 + slot * 2 + h
                    pool.tensor_copy(pb[:, rt:rt + 2, bass.ds(head, 1)], pr[:, k % 2, :, SEQ:TOK]).then_inc(s_pb, 1)
                    g = k // 8
                    if not (last and g == 1):
                        n = L * GROUPS + j * 2 + g + 1
                        if k % 8 == 0:
                            split_v(n, (g + 1) % 2)
                        if k % 8 == 1:
                            split_q(n, (g + 1) % 2)
                        if k % 8 == 2:
                            split_k(n, (g + 1) % 2)
                        if k % 8 == 6:
                            split_o(n, (g + 1) % 2)

            with pool.Fori(0, LAYERS) as L:
                split_v(L * GROUPS, 0)
                split_q(L * GROUPS, 0)
                split_k(L * GROUPS, 0)
                key_bias(L, 0, 0)
                split_o(L * GROUPS, 0)
                body(L, 0, first=True)
                with pool.Fori(1, BODIES - 1) as j:
                    body(L, j)
                body(L, BODIES - 1, last=True)

            pool.wait_ge(d_w1, 16)
            pool.wait_ge(d_w2, 16)
            pool.nop(nofuse=True)
            for i in range(8):
                raw, H, Lo = (w1raw, w1H, w1L) if i < 4 else (w2raw, w2H, w2L)
                c = slice(i % 4 * 512, (i % 4 + 1) * 512)
                split(raw[:, c], H[:, c], Lo[:, c], i + 1, m_whi, m_w)


def _by_partition(a):
    n = a.shape[0] // P
    return np.ascontiguousarray(a.reshape(n, P, a.shape[1]).transpose(1, 0, 2)).reshape(P, -1)


def _layout(i):
    f = {k: np.asarray(v) for k, v in i.items()}
    x_rows = f["x"].reshape(ROWS, HID)
    ctx_rows = f["ctx_2048"].reshape(ROWS, HID)
    pre = "L1_xattn_"

    cols = []
    for g, b in (("L0_xattn_ln_gamma", "L0_xattn_ln_beta"), (pre + "ln1_scale", pre + "ln1_offset"),
                 (pre + "ln2_scale", pre + "ln2_offset"), (pre + "ln_mlp_scale", pre + "ln_mlp_offset")):
        cols += [f[g].reshape(KT, P).T, f[b].reshape(KT, P).T]
    cols.append(np.broadcast_to(f["L0_xattn_gate"].reshape(1, 1), (P, 1)))
    cols.append(f[pre + "b_fc1"].reshape(FT, P).T)
    own = (np.arange(P)[:, None] // HD0) % HG0 == np.arange(HG0)[None, :]
    cols.append(np.where(own, np.float32(1), np.float32(0)))
    cols = np.ascontiguousarray(np.concatenate(cols, axis=1))

    def twice(w):
        t = w.T.reshape(KT, P, NG0, 1, HG0 * HD0)
        return np.broadcast_to(t, (KT, P, NG0, 2, HG0 * HD0)).transpose(1, 0, 2, 3, 4).reshape(P, -1)

    wo = f["L0_xattn_Wo"].T.reshape(NG0, HG0, 1, HD0, HID)
    wo = np.broadcast_to(wo, (NG0, HG0, 2, HD0, HID)).transpose(1, 2, 3, 0, 4).reshape(P, -1)
    w0 = np.ascontiguousarray(np.concatenate(
        [twice(f["L0_xattn_Wq"]), twice(f["L0_xattn_Wk"]), _by_partition(f["L0_xattn_Wv"].T), wo], axis=1))

    wg = np.zeros((LAYERS, GROUPS, P, C_END), np.float32)
    bo18 = np.zeros((BWR, LAYERS, HID), np.float32)
    for n in range(LAYERS):
        get = lambda name: f[f"{pre}{name}{n + 1}"]
        for g in range(GROUPS):
            w = wg[n, g]
            s = slice(g * GW, (g + 1) * GW)
            for c, name in ((C_V, "wv"), (C_Q, "wq"), (C_K, "wk")):
                w[:, c:c + 512] = _by_partition(get(name)[:, s])
            w[:, C_O:C_BV] = _by_partition(get("wo")[s])
            for h in range(GH):
                head = g * GH + h
                d = slice(head * HD, (head + 1) * HD)
                w[:, C_SMALL + h] = get("bq")[d]
                w[:, C_SMALL + 2 + h] = get("bk")[d]
                w[:, C_SMALL + 4 + h] = get("bias_k")[0, 0, head]
                a, b = C_BV + h * BWR, C_BV + (GH + h) * BWR
                w[:, a + head] = get("bias_v")[0, 0, head]
                w[:, a + HEADS] = get("bv")[d]
                w[:, b + head] = get("bv")[d]
        bo18[HEADS + 1, n] = get("bo")
    mask = f["mask_BxS2_bf1"].reshape(1, ROWS).view(np.uint8)
    return {
        "x_rows": x_rows, "x_t": _by_partition(x_rows.T), "ctx_rows": ctx_rows, "ctx_t": _by_partition(ctx_rows.T),
        "mask_rows": np.ascontiguousarray(np.broadcast_to(mask, (P, ROWS))), "cols": cols,
        "ident_in": np.eye(P, dtype=np.float32), "w0": w0, "wg": wg.reshape(LAYERS * GROUPS, P, C_END), "bo18": bo18,
        "w1": _by_partition(f[pre + "w_fc1"]), "w2": _by_partition(f[pre + "w_fc2"]),
        "b2": np.ascontiguousarray(np.broadcast_to(f[pre + "b_fc2"].reshape(1, HID), (P, HID))),
    }


def kernel(**inputs):
    import concourse.bacc as bacc
    from concourse.bass_utils import run_bass_kernel_spmd

    nc = bacc.Bacc("TRN2", target_bir_lowering=False, num_devices=1)
    arrays, args = {}, {}
    for name, a in _layout(inputs).items():
        a = np.ascontiguousarray(a)
        arrays[name] = a
        args[name] = nc.dram_tensor(name, a.shape, mybir.dt.from_np(a.dtype), kind="ExternalInput").ap()
    out = nc.dram_tensor("out", (ROWS, HID), F32, kind="ExternalOutput").ap()
    build_program(nc, **args, out=out)
    r = run_bass_kernel_spmd(nc, [arrays], core_ids=[0])
    return r.results[0]["out"].reshape(BATCH, SEQ, HID)
```

```python
from contextlib import ExitStack

import numpy as np
import concourse.bass as bass
from concourse import mybir
from concourse.alu_op_type import AluOpType as ALU

ACT = mybir.ActivationFunctionType
F32 = mybir.dt.float32
F32R = mybir.dt.float32r
U8 = mybir.dt.uint8
AX_X = mybir.AxisListType.X

P = 128
BATCH, SEQ, HID = 4, 256, 256
KT = HID // P
ROWS = BATCH * SEQ
RT = ROWS // P
HEADS = 16
EPS = 1e-5

HD0 = HID // HEADS
HG0 = 4
NG0 = HEADS // HG0
SCALE0 = float(HD0) ** -0.5

LAYERS = 2
HD = 128
GH = 2
GROUPS = HEADS // GH
GW = GH * HD
SCALE = float(HD) ** -0.5
TOK = SEQ + 1
KW = SEQ + 2
BWR = HEADS + 2
STEPS = 16
BODIES = HEADS * BATCH // STEPS
WO_LAG = 6
TAIL = 3
T_LAG0, PV_LAG0 = 3, 5
TAIL0 = 7
FF = 1024
FT = FF // P

C_V, C_Q, C_K, C_SMALL, C_O, C_BV, C_END = 0, 512, 1024, 1536, 1542, 2054, 2054 + 2 * GH * BWR
C_LN, C_GATE, C_B1, C_MASK, C_COLS = 0, 16, 17, 25, 29
C0_Q, C0_K, C0_V, C0_O, C0_END = 0, 1024, 2048, 2560, 3584


def first_body(j):
    return isinstance(j, int) and j == 0


def build_program(nc, x_rows, x_t, ctx_rows, ctx_t, mask_rows, cols, ident_in, w0, wg, bo18, w2, b2, out):
    with ExitStack() as ctx:
        def sb(name, shape, dt=F32, on=ctx):
            return on.enter_context(nc.sbuf_tensor(name, shape, dt))

        def sem(name):
            return ctx.enter_context(nc.semaphore(name))

        bank = [ctx.enter_context(nc.psum_tensor(f"bank{i}", [P, 512], F32)) for i in range(8)]

        prm = sb("prm", [P, C_COLS])
        ident = sb("ident", [P, P])
        x = sb("x", [P, RT, HID])
        ctxH, ctxL = sb("ctxH", [P, KT, ROWS], F32R), sb("ctxL", [P, KT, ROWS], F32R)
        hH, hL = sb("hH", [P, KT, ROWS], F32R), sb("hL", [P, KT, ROWS], F32R)
        ln_st = sb("ln_st", [P, RT, 6])
        ln_mv = sb("ln_mv", [P, RT, 2])
        ln_sd = sb("ln_sd", [P, RT])
        ln_rs = sb("ln_rs", [P, RT])
        xn = sb("xn", [P, RT, HID])
        ln_y = sb("ln_y", [P, 2, 512])
        stage = sb("stage", [P, C_END])
        early = ctx.enter_context(ExitStack())
        xt_raw, ct_raw = sb("xt_raw", [P, KT * ROWS], F32, early), sb("ct_raw", [P, KT * ROWS], F32, early)
        early.close()
        wH, wL = [sb("wH0", [P, 2048], F32R)], [sb("wL0", [P, 2048], F32R)]
        small = sb("small", [P, 2, 6])
        kbH, kbL = sb("kbH", [P, 2, GH], F32R), sb("kbL", [P, 2, GH], F32R)
        bv = sb("bv", [P, GH * BWR])
        bvH, bvL = sb("bvH", [P, 2, GH * BWR], F32R), sb("bvL", [P, 2, GH * BWR], F32R)
        unread = sb("unread", [P, 1])
        mx = sb("mx", [P, 2, 2])
        nb = sb("nb", [P, 4, 2])
        sm = sb("sm", [P, 4, 2])
        rs = sb("rs", [P, 4, 2])

        l0 = ctx.enter_context(ExitStack())
        w0H, w0L = sb("w0H", [P, C0_END], F32R, l0), sb("w0L", [P, C0_END], F32R, l0)
        q0 = sb("q0", [P, NG0, ROWS], F32, l0)
        k0H, k0L = sb("k0H", [P, NG0, ROWS], F32R, l0), sb("k0L", [P, NG0, ROWS], F32R, l0)
        v0 = sb("v0", [P, RT, HID], F32, l0)
        mask8 = sb("mask8", [P, ROWS], U8, l0)
        maskb = sb("maskb", [P, ROWS], F32, l0)
        maskc = sb("maskc", [P, SEQ], F32, l0)
        raws = l0.enter_context(ExitStack())
        w0raw = sb("w0raw", [P, C0_END], F32, raws)
        c_rows = sb("c_rows", [P, RT, HID], F32, raws)
        anH, anL = sb("anH", [P, KT, ROWS], F32R, raws), sb("anL", [P, KT, ROWS], F32R, raws)
        raws.close()
        q0m = sb("q0m", [P, 4, SEQ], F32R, l0)
        s0 = sb("s0", [P, 2, 2, SEQ], F32, l0)
        p0 = sb("p0", [P, 4, 2, SEQ], F32, l0)
        a0H, a0L = sb("a0H", [P, NG0, SEQ], F32R, l0), sb("a0L", [P, NG0, SEQ], F32R, l0)
        pt0H, pt0L = sb("pt0H", [P, 2, 512], F32R, l0), sb("pt0L", [P, 2, 512], F32R, l0)
        l0.close()

        v0p = [h[:, :, :].rearrange("p k (a c) -> p (k a) c", c=P) for h in (hH, hL)]

        w2raw = sb("w2raw", [P, FT * HID])
        w2H, w2L = sb("w2H", [P, FT * HID], F32R), sb("w2L", [P, FT * HID], F32R)
        b2b = sb("b2b", [P, HID])
        wH.append(sb("wH1", [P, 2048], F32R))
        wL.append(sb("wL1", [P, 2048], F32R))
        l1 = ctx.enter_context(ExitStack())
        qH, qL = sb("qH", [P, 2, 512], F32R, l1), sb("qL", [P, 2, 512], F32R, l1)
        kH, kL = sb("kH", [P, 2, 2, KW], F32R, l1), sb("kL", [P, 2, 2, KW], F32R, l1)
        vH, vL = sb("vH", [P, 2, 4, GW], F32R, l1), sb("vL", [P, 2, 4, GW], F32R, l1)
        aH, aL = sb("aH", [P, 2, GH, 512], F32R, l1), sb("aL", [P, 2, GH, 512], F32R, l1)
        pr = sb("pr", [P, 2, 2, TOK], F32, l1)
        ptH, ptL = sb("ptH", [P, 2, 512], F32R, l1), sb("ptL", [P, 2, 512], F32R, l1)
        pb = sb("pb", [P, RT, BWR], F32, l1)
        pbT = sb("pbT", [BWR, ROWS], F32, l1)
        bo = sb("bo", [BWR, LAYERS, HID], F32, l1)
        bw = sb("bw", [BWR, HID], F32, l1)
        l1.close()
        gel = sb("gel", [P, 2, 512])
        gH, gL = sb("gH", [P, FT, ROWS], F32R), sb("gL", [P, FT, ROWS], F32R)
        res = sb("res", [P, RT, HID])

        d_prm, d_ident, d_crows, d_w0, d_xt, d_ct, d_x, d_mask = [
            sem(n) for n in ("d_prm", "d_ident", "d_crows", "d_w0", "d_xt", "d_ct", "d_x", "d_mask")]
        d_wa, d_wo, d_bo, d_w2, d_b2, d_out, d_w0q, d_xt2 = [
            sem(n) for n in ("d_wa", "d_wo", "d_bo", "d_w2", "d_b2", "d_out", "d_w0q", "d_xt2")]
        ln_stat, ln_agg, ln_sqrt, ln_rcp, ln_xn, ln_tr, ln_y_done, ln_hi, ln_lo = [
            sem(n) for n in ("ln_stat", "ln_agg", "ln_sqrt", "ln_rcp", "ln_xn", "ln_tr", "ln_y_done", "ln_hi", "ln_lo")]
        sp_hi, sp_lo, c_hi, c_lo = sem("sp_hi"), sem("sp_lo"), sem("c_hi"), sem("c_lo")
        mask_s, mask_ready, v0p_zero = sem("mask_s"), sem("mask_ready"), sem("v0p_zero")
        v0_cp = sem("v0_cp")
        gate_t = sem("gate_t")
        pj_mm, pj_hi, pj_lo = sem("pj_mm"), sem("pj_hi"), sem("pj_lo")
        vp_hi, vp_lo, mk_cp = sem("vp_hi"), sem("vp_lo"), sem("mk_cp")
        g_qm, g_s, g_max, g_exp, g_rs, g_norm = [
            sem(n) for n in ("g_qm", "g_s", "g_max", "g_exp", "g_rs", "g_norm")]
        g_t, g_pth, g_ptl, g_pv, g_ah, g_al, g_wo, g_add = [
            sem(n) for n in ("g_t", "g_pth", "g_ptl", "g_pv", "g_ah", "g_al", "g_wo", "g_add")]
        w_hi_b = sem("w_hi_b")
        w_hi, w_v, w_q, w_k, w_o, bv_d = sem("w_hi"), sem("w_v"), sem("w_q"), sem("w_k"), sem("w_o"), sem("bv_d")
        kb_cp, pb_ones = sem("kb_cp"), sem("pb_ones")
        s_mm, s_max, s_nb, s_exp, s_rs, s_norm, s_pb = [
            sem(n) for n in ("s_mm", "s_max", "s_nb", "s_exp", "s_rs", "s_norm", "s_pb")]
        t_mm, pt_hi, pt_lo, pv_mm, a_hi, a_lo = [
            sem(n) for n in ("t_mm", "pt_hi", "pt_lo", "pv_mm", "a_hi", "a_lo")]
        v_mm, v_hi, v_lo, o_mm, x_add = [sem(n) for n in ("v_mm", "v_hi", "v_lo", "o_mm", "x_add")]
        q_mm, q_hi, q_lo, k_mm, k_hi, k_lo = [sem(n) for n in ("q_mm", "q_hi", "q_lo", "k_mm", "k_hi", "k_lo")]
        bw_mm, bw_add, pbt_mm, pbt_cp = [sem(n) for n in ("bw_mm", "bw_add", "pbt_mm", "pbt_cp")]
        m_whi, m_w, m_xb, f1_mm, f1_gelu, f1_hi, f1_lo, f2_mm, f2_add = [
            sem(n) for n in ("m_whi", "m_w", "m_xb", "f1_mm", "f1_gelu", "f1_hi", "f1_lo", "f2_mm", "f2_add")]

        as_f32 = lambda ap: ap.bitcast(F32)

        def three_passes(pe, dst, lhs, rhs, first, last):
            pe.matmul(dst, lhs[0], rhs[0], start=first, stop=False)
            pe.matmul(dst, lhs[0], rhs[1], start=False, stop=False)
            return pe.matmul(dst, lhs[1], rhs[0], start=False, stop=last)

        SPLITS = [("xt", 0), ("xt", ROWS), ("w0", C0_Q), ("w0", C0_Q + 512), ("xt", 512), ("xt", ROWS + 512)]

        def split_aps(what, c):
            if what == "xt":
                kt, r = divmod(c, ROWS)
                return xt_raw[:, c:c + 512], hH[:, kt, r:r + 512], hL[:, kt, r:r + 512]
            return w0raw[:, c:c + 512], w0H[:, c:c + 512], w0L[:, c:c + 512]

        def projected(i):
            return bank[4 + i % 4 if i < 8 else (4 + i) % 8]

        def v0_part(b, t, g):
            return v0[:, bass.ds(b * 2 + t, 1), g * HG0 * HD0:(g + 1) * HG0 * HD0].rearrange(
                "p t (j d) -> p (t j) d", j=HG0)

        def v0p_part(t, g, lo):
            v = v0p[t][:, g * HG0:(g + 1) * HG0, :]
            return bass.AP(tensor=v.tensor, offset=v.offset + lo * HD0,
                           ap=[list(v.ap[0]), [P + 2 * HD0, HG0], [1, HD0]])

        def step(k):
            return (k // 8) % 2, (k // 4) % 2, (k // 2) % 2, k % 2

        def outputs_at(k, first, last):
            if last and k >= 14:
                return {14: (8,), 15: (9, 10), 16: (11,), 17: (12, 13), 18: (14, 15)}.get(k, ())
            return () if first and k < WO_LAG else (k - WO_LAG,)

        def value_bank(j, m):
            return {1: bank[2], 3: bank[3]}.get(m, bank[6]) if first_body(j) else bank[6]

        def gated_outputs_at(k, first):
            if k >= HEADS:
                return {17: (0, 1), 18: (2, 3), 19: (4, 5), 22: (6, 7)}.get(k, ())
            return (k - 5,) if 5 <= k < 13 and not first else ()

        def output_bank(m, last):
            return bank[4] if last and m >= 8 and m % 2 == 1 else bank[7]

        block = ctx.enter_context(nc.Block())

        @block.sync
        def _(sp):
            halves = [(xt_raw[:, :].rearrange("p (k r) -> p k r", k=KT)[:, :, h * 512:h * 512 + 512],
                       x_t.rearrange("p (k r) -> p k r", k=KT)[:, :, h * 512:h * 512 + 512]) for h in range(2)]
            sp.dma_start(*halves[0]).then_inc(d_xt, 16)
            sp.dma_start(w0raw[:, C0_Q:C0_K], w0[:, C0_Q:C0_K]).then_inc(d_w0q, 16)
            sp.dma_start(*halves[1]).then_inc(d_xt2, 16)
            sp.dma_start(mask8[:, :], mask_rows).then_inc(d_mask, 16)
            sp.dma_start(prm[:, :], cols).then_inc(d_prm, 16)
            sp.dma_start(ident[:, :], ident_in).then_inc(d_ident, 16)
            sp.dma_start(c_rows[:, :, :], ctx_rows.rearrange("(r p) c -> p r c", p=P)).then_inc(d_crows, 16)
            sp.dma_start(w0raw[:, C0_K:C0_END], w0[:, C0_K:C0_END]).then_inc(d_w0, 16)
            sp.dma_start(ct_raw[:, :], ctx_t).then_inc(d_ct, 16)
            sp.dma_start(x[:, :, :], x_rows.rearrange("(r p) c -> p r c", p=P)).then_inc(d_x, 16)
            sp.dma_start(stage[:, 0:C_O], wg[0, :, 0:C_O]).then_inc(d_wa, 16)
            sp.dma_start(stage[:, C_O:C_END], wg[0, :, C_O:C_END]).then_inc(d_wo, 16)
            sp.wait_ge(g_add, 2 * BATCH)
            sp.dma_start(bo[:, :, :], bo18).then_inc(d_bo, 16)
            sp.dma_start(w2raw[:, :], w2).then_inc(d_w2, 16)
            sp.dma_start(b2b[:, :], b2).then_inc(d_b2, 16)
            with sp.Fori(1, LAYERS * GROUPS + 1) as n:
                sp.wait_ge(w_k, n)
                sp.dma_start(stage[:, 0:C_O], wg[n, :, 0:C_O]).then_inc(d_wa, 16)
                sp.wait_ge(w_o, n)
                sp.dma_start(stage[:, C_O:C_END], wg[n, :, C_O:C_END]).then_inc(d_wo, 16)
            for r in range(RT):
                sp.wait_ge(f2_add, r + 1)
                sp.dma_start(out[r * P:(r + 1) * P, :], res[:, r, :]).then_inc(d_out, 16)
            sp.wait_ge(d_out, 16 * RT)

        @block.tensor
        def _(pe):
            def ln_transposes(n, half):
                pe.wait_ge(ln_xn, n * RT + 4 * half + 4)
                for kt in range(KT):
                    for i in range(4):
                        mm = pe.transpose(bank[2 * half + kt][:, i * P:(i + 1) * P],
                                          xn[:, 4 * half + i, kt * P:(kt + 1) * P], ident[:, :])
                    mm.then_inc(ln_tr, 1)

            def proj_bank(i):
                if 4 <= i < 12:
                    pe.wait_ge(pj_lo, i - 3)
                elif 12 <= i < 16:
                    pe.wait_ge(ln_y_done, i - 11)
                elif i >= 16:
                    pe.wait_ge(pj_lo, i - 7)
                return projected(i)

            def project(i, c0, inH, inL):
                half, g = divmod(i % 8, NG0)
                dst = proj_bank(i)
                for kt in range(KT):
                    c = c0 + kt * 512 + g * P
                    r = slice(half * 512, half * 512 + 512)
                    mm = three_passes(pe, dst[:, :], (w0H[:, c:c + P], w0L[:, c:c + P]),
                                      (inH[:, kt, r], inL[:, kt, r]), kt == 0, kt == KT - 1)
                mm.then_inc(pj_mm, 1)

            pe.wait_ge(sp_lo, 4)
            for i in range(8):
                if i == NG0:
                    pe.wait_ge(sp_lo, 6)
                if i == 6:
                    pe.wait_ge(d_ident, 16)
                    ln_transposes(0, 0)
                project(i, C0_Q, hH, hL)
            ln_transposes(0, 1)
            pe.wait_ge(c_lo, 3)
            for half in range(2):
                pe.wait_ge(ln_lo, 2 + 2 * half)
                for g in range(NG0):
                    project(8 + half * NG0 + g, C0_K, anH, anL)
            for i in range(RT):
                dst = proj_bank(16 + i)
                for kt in range(KT):
                    c = C0_V + kt * HID
                    r = slice(i * P, i * P + P)
                    mm = three_passes(pe, dst[:, 0:HID], (anH[:, kt, r], anL[:, kt, r]),
                                      (w0H[:, c:c + HID], w0L[:, c:c + HID]), kt == 0, kt == KT - 1)
                mm.then_inc(pj_mm, 1)
            pe.wait_ge(c_lo, 5)
            pe.wait_ge(pj_lo, 16)
            pe.wait_ge(v0_cp, 6)

            def gated_batch(b, first=False, last=False):
                for k in range(HEADS + (TAIL0 if last else 0)):
                    if k < HEADS:
                        pe.wait_ge(g_qm, b * HEADS + k + 1)
                        if not (first and k < 2):
                            pe.wait_ge(g_max, b * HEADS + k - 1)
                        for qt in range(2):
                            lhs = q0m[:, k % 4, qt * P:(qt + 1) * P]
                            dst = bank[k % 2][:, qt * SEQ:(qt + 1) * SEQ]
                            pe.matmul(dst, lhs, k0H[:, k // HG0, bass.ds(b * SEQ, SEQ)], start=True, stop=False)
                            mm = pe.matmul(dst, lhs, k0L[:, k // HG0, bass.ds(b * SEQ, SEQ)], start=False, stop=True)
                        mm.then_inc(g_s, 1)
                    for c in gated_outputs_at(k, first):
                        g, qt = divmod(c, 2)
                        before = NG0 if k < HEADS else 0
                        pe.wait_ge(g_al, b * NG0 - before + g + 1)
                        if k >= HEADS and g == 0:
                            pe.wait_ge(g_add, b * 2 - 1 + qt)
                        q = slice(qt * P, (qt + 1) * P)
                        w = C0_O + g * HID
                        mm = three_passes(pe, bank[6 + qt][:, 0:HID], (a0H[:, g, q], a0L[:, g, q]),
                                          (w0H[:, w:w + HID], w0L[:, w:w + HID]), g == 0, g == NG0 - 1)
                        if g == NG0 - 1:
                            mm.then_inc(g_wo, 1)
                    m = k - PV_LAG0
                    if (m >= 0 or not first) and m < HEADS:
                        n, head = b * HEADS + m, m % HEADS
                        g = head // HG0
                        if head % HG0 == 0:
                            pe.wait_ge(vp_lo, b * NG0 + m // HG0 + 1)
                            if not (first and m < 2 * HG0):
                                pe.wait_ge(g_al, b * NG0 + m // HG0 - 1)
                        pe.wait_ge(g_ptl, n + 1)
                        for tt in range(2):
                            for i, src in enumerate((pt0H, pt0L)):
                                mm = pe.matmul(bank[4 + g % 2][:, 0:SEQ], v0p[tt][:, head, :],
                                               src[:, head % 2, tt * SEQ:(tt + 1) * SEQ],
                                               start=(head % HG0 == 0 and tt == 0 and i == 0),
                                               stop=(head % HG0 == HG0 - 1 and tt == 1 and i == 1))
                        mm.then_inc(g_pv, 1)
                    m = k - T_LAG0
                    if (m >= 0 or not first) and m < HEADS:
                        n = b * HEADS + m
                        pe.wait_ge(g_norm, n + 1)
                        if first and m < 2:
                            pe.wait_ge(v0_cp, 8)
                        else:
                            pe.wait_ge(g_ptl, n - 1)
                        for tt in range(2):
                            for qt in range(2):
                                mm = pe.transpose(bank[2 + m % 2][:, tt * SEQ + qt * P:tt * SEQ + (qt + 1) * P],
                                                  p0[:, m % 4, qt, tt * P:(tt + 1) * P], ident[:, :])
                        mm.then_inc(g_t, 1)

            gated_batch(0, first=True)
            with pe.Fori(1, BATCH - 1) as b:
                gated_batch(b)
            gated_batch(BATCH - 1, last=True)

            pe.wait_ge(g_add, 2 * BATCH)

            def weights(part, slot, c, n):
                o = {"v": 0, "q": 512, "k": 1024, "o": 1536}[part] + c
                return wH[slot][:, o:o + n], wL[slot][:, o:o + n]

            def project_v(L, j, m):
                slot, bp = (m // 8) % 2, (m // 4) % 2
                if m % 8 == 0:
                    pe.wait_ge(w_v, L * GROUPS + j * 2 + m // 8 + 1)
                if not (first_body(j) and m in (0, 1, 3)):
                    before = 1 if first_body(j) and m < 5 else 0
                    pe.wait_ge(v_lo, L * 64 + j * STEPS + m - before)
                r = slice((bp * 4 + m % 4) * P, (bp * 4 + m % 4 + 1) * P)
                for kt in range(KT):
                    mm = three_passes(pe, value_bank(j, m)[:, 0:GW], (ctxH[:, kt, r], ctxL[:, kt, r]),
                                      weights("v", slot, kt * GW, GW), kt == 0, kt == KT - 1)
                mm.then_inc(v_mm, 1)

            def project_qk(L, j, u, is_q):
                slot, bp, h = (u // 4) % 2, (u // 2) % 2, u % 2
                ready, free, done, to = (w_q, q_lo, q_mm, 4) if is_q else (w_k, k_lo, k_mm, 5)
                if is_q and u == 2 and first_body(j):
                    pe.wait_ge(ln_lo, (L + 1) * 4 + 4)
                if u % 4 == 0:
                    pe.wait_ge(ready, L * GROUPS + j * 2 + u // 4 + 1)
                if not (first_body(j) and u == 0):
                    pe.wait_ge(free, L * 32 + j * 8 + u)
                inH, inL = (hH, hL) if is_q else (ctxH, ctxL)
                r = slice(bp * 512, bp * 512 + 512)
                for kt in range(KT):
                    if is_q and u == 0 and first_body(j):
                        pe.wait_ge(ln_lo, (L + 1) * 4 + kt + 1)
                    mm = three_passes(pe, bank[to][:, :], weights("q" if is_q else "k", slot, kt * GW + h * HD, HD),
                                      (inH[:, kt, r], inL[:, kt, r]), kt == 0, kt == KT - 1)
                mm.then_inc(done, 1)

            def scores(L, j, k):
                slot = (k // 2) % 2
                if k % 2 == 0:
                    pe.wait_ge(q_lo, L * 32 + j * 8 + k // 2 + 1)
                    pe.wait_ge(k_lo, L * 32 + j * 8 + k // 2 + 1)
                    pe.wait_ge(kb_cp, L * 32 + j * 8 + k // 2 + 1)
                if not (first_body(j) and k == 0):
                    pe.wait_ge(s_exp, L * 64 + j * STEPS + k)
                b = k % 2
                for qt in range(2):
                    q = slice(b * SEQ + qt * P, b * SEQ + (qt + 1) * P)
                    mm = three_passes(pe, bank[qt][:, 0:KW], (qH[:, slot, q], qL[:, slot, q]),
                                      (kH[:, slot, b, :], kL[:, slot, b, :]), True, True)
                mm.then_inc(s_mm, 1)

            def values(L, j, k):
                slot, bp, h, b = step(k)
                vs = (k // 4) % 2
                pe.wait_ge(pt_lo, L * 64 + j * STEPS + k + 1)
                pe.wait_ge(v_lo, L * 64 + j * STEPS + k // 4 * 4 + b * 2 + 2)
                if first_body(j) and k == 0:
                    pe.wait_ge(ln_y_done, (L + 1) * 4 + 4)
                else:
                    pe.wait_ge(a_lo, L * 64 + j * STEPS + k)
                for tt in range(2):
                    d = slice(h * HD, (h + 1) * HD)
                    t = slice(tt * SEQ, (tt + 1) * SEQ)
                    mm = three_passes(pe, bank[3][:, 0:SEQ], (vH[:, vs, b * 2 + tt, d], vL[:, vs, b * 2 + tt, d]),
                                      (ptH[:, k % 2, t], ptL[:, k % 2, t]), tt == 0, tt == 1)
                mm.then_inc(pv_mm, 1)

            def transposes(L, j, k):
                pe.wait_ge(s_norm, L * 64 + j * STEPS + k + 1)
                if first_body(j) and k == 0:
                    pe.wait_ge(ln_y_done, (L + 1) * 4 + 3)
                else:
                    pe.wait_ge(pt_lo, L * 64 + j * STEPS + k)
                for tt in range(2):
                    for qt in range(2):
                        mm = pe.transpose(bank[2][:, tt * SEQ + qt * P:tt * SEQ + (qt + 1) * P],
                                          pr[:, k % 2, qt, tt * P:(tt + 1) * P], ident[:, :])
                mm.then_inc(t_mm, 1)

            def output(L, j, m, last):
                slot, vs, i = (m // 8) % 2, (m // 4) % 2, m % 4
                b = i // 2
                if m % 8 == 0:
                    pe.wait_ge(w_o, L * GROUPS + j * 2 + m // 8 + 1)
                if last and m >= 8:
                    pe.wait_ge(x_add, L * 64 + j * STEPS + (m - 1 if m >= 10 else 8))
                elif not (first_body(j) and m == 0):
                    pe.wait_ge(x_add, L * 64 + j * STEPS + m)
                k = m + WO_LAG
                if k < STEPS and k % 8 == 0 or (first_body(j) and m == 0):
                    pe.wait_ge(bw_add, L * GROUPS + j * 2 + k // 8 + 1)
                dst, bias = output_bank(m, last)[:, 0:HID], last and m >= 8
                if bias:
                    rt = m - 8
                    pe.wait_ge(pbt_cp, L * 2 + rt // 4 + 1)
                    pe.matmul(dst, pbT[:, rt * P:(rt + 1) * P], bw[:, :], start=True, stop=False)
                pe.wait_ge(a_lo, L * 64 + j * STEPS + m // 4 * 4 + 3 + b)
                for h in range(GH):
                    q = slice(i * P, (i + 1) * P)
                    mm = three_passes(pe, dst, (aH[:, vs, h, q], aL[:, vs, h, q]),
                                      weights("o", slot, h * HID, HID), h == 0 and not bias, h == GH - 1)
                mm.then_inc(o_mm, 1)

            def bias_product(L, j, g):
                pe.wait_ge(w_o, L * GROUPS + j * 2 + g + 1)
                if not (first_body(j) and g == 0):
                    pe.wait_ge(x_add, L * 64 + j * STEPS + 8 * g - WO_LAG)
                for h in range(GH):
                    c = slice(h * BWR, (h + 1) * BWR)
                    mm = three_passes(pe, bank[7][0:BWR, 0:HID], (bvH[:, g, c], bvL[:, g, c]),
                                      weights("o", g, h * HID, HID), h == 0, h == GH - 1)
                mm.then_inc(bw_mm, 1)

            def bias_token(L, half):
                pe.wait_ge(s_pb, L * 64 + 60 + 4 * half)
                pe.wait_ge(v_lo, L * 64 + 64)
                if half == 1:
                    pe.wait_ge(pbt_cp, L * 2 + 1)
                for i in range(4):
                    mm = pe.transpose(bank[6][0:BWR, i * P:(i + 1) * P], pb[:, 4 * half + i, :], ident[:, :])
                mm.then_inc(pbt_mm, 1)

            def body(L, j, first=False, last=False):
                for k in range(STEPS + (TAIL if last else 0)):
                    if k < STEPS:
                        scores(L, j, k)
                    if first and k == 0:
                        ln_transposes(L + 1, 1)
                        project_qk(L, j, 1, True)
                    if k < STEPS and not (first and k < 2) and not (last and k // 2 + 1 >= STEPS // 2):
                        project_qk(L, j, k // 2 + 1, k % 2 == 0)
                    if last and k in (13, 17):
                        bias_token(L, (k - 13) // 4)
                    if (k >= 2 or not first) and k - 2 < STEPS:
                        values(L, j, k - 2)
                    if k < STEPS and k % 8 == 0 and not (first and k == 0):
                        bias_product(L, j, k // 8)
                    if (k >= 1 or not first) and k - 1 < STEPS:
                        transposes(L, j, k - 1)
                    if k < STEPS and not (first and k == 0) and not (last and k + 4 >= STEPS):
                        project_v(L, j, k + 4)
                    for m in outputs_at(k, first, last):
                        output(L, j, m, last)

            pe.wait_ge(c_lo, 9)
            with pe.Fori(0, LAYERS) as L:
                project_v(L, 0, 0)
                ln_transposes(L + 1, 0)
                project_v(L, 0, 1)
                project_qk(L, 0, 0, False)
                project_v(L, 0, 2)
                project_v(L, 0, 3)
                project_qk(L, 0, 0, True)
                project_qk(L, 0, 1, False)
                bias_product(L, 0, 0)
                project_v(L, 0, 4)
                body(L, 0, first=True)
                with pe.Fori(1, BODIES - 1) as j:
                    body(L, j)
                body(L, BODIES - 1, last=True)

            ln_transposes(LAYERS + 1, 0)
            pe.wait_ge(w_o, LAYERS * GROUPS + 1)
            for i in range(2 * FT):
                if i == 4:
                    ln_transposes(LAYERS + 1, 1)
                half, f = divmod(i, FT)
                if i >= 2:
                    pe.wait_ge(f1_gelu, i - 1)
                for kt in range(KT):
                    if f == 0:
                        pe.wait_ge(ln_lo, (LAYERS + 1) * 4 + 2 * half + kt + 1)
                    c = slice(kt * FF + f * P, kt * FF + (f + 1) * P)
                    r = slice(half * 512, half * 512 + 512)
                    mm = three_passes(pe, bank[4 + i % 2][:, :], (wH[0][:, c], wL[0][:, c]),
                                      (hH[:, kt, r], hL[:, kt, r]), kt == 0, kt == KT - 1)
                mm.then_inc(f1_mm, 1)
            pe.wait_ge(m_w, 4)
            for r in range(RT):
                pe.wait_ge(f1_lo, (r // 4 + 1) * FT)
                if r >= 2:
                    pe.wait_ge(f2_add, r - 1)
                for f in range(FT):
                    q = slice(r * P, (r + 1) * P)
                    c = slice(f * HID, (f + 1) * HID)
                    mm = three_passes(pe, bank[6 + r % 2][:, 0:HID], (gH[:, f, q], gL[:, f, q]),
                                      (w2H[:, c], w2L[:, c]), f == 0, f == FT - 1)
                mm.then_inc(f2_mm, 1)

        @block.scalar
        def _(act):
            def load_table(func):
                act.activation(unread[:, :], prm[:, C_MASK:C_MASK + 1], func)

            def ln_sqrts(n, half):
                act.wait_ge(ln_agg, n * 4 + 2 * half + 2)
                h = slice(4 * half, 4 * half + 4)
                act.activation(ln_sd[:, h], ln_sd[:, h], ACT.Sqrt).then_inc(ln_sqrt, 1)

            def ln_his(n, half, kts=range(KT)):
                for kt in kts:
                    u = 2 * half + kt
                    act.wait_ge(ln_tr, n * 4 + u + 1)
                    if not (first_body(n) and half == 0):
                        act.wait_ge(ln_lo, n * 4 + u - 1)
                    act.nop(nofuse=True)
                    c = C_LN + n * 4 + kt
                    act.activation(ln_y[:, kt, :], bank[2 * half + kt][:, :], ACT.Identity,
                                   bias=prm[:, bass.ds(c + 2, 1)], scale=prm[:, bass.ds(c, 1)]).then_inc(ln_y_done, 1)
                    act.wait_ge(ln_y_done, n * 4 + u + 1)
                    dst = (anH if first_body(n) else hH)[:, kt, half * 512:half * 512 + 512]
                    act.activation(dst, ln_y[:, kt, :], ACT.Copy).then_inc(ln_hi, 1)

            def split_his(parts):
                for what, c in parts:
                    src, hi, _ = split_aps(what, c)
                    act.activation(hi, src, ACT.Copy).then_inc(sp_hi, 1)

            def project_hi(i):
                act.wait_ge(pj_mm, i + 1)
                half, g = divmod(i % 8, NG0)
                dst = (q0 if i < 8 else k0H)[:, g, half * 512:half * 512 + 512]
                act.activation(dst.bitcast(F32R), projected(i)[:, :], ACT.Copy).then_inc(pj_hi, 1)

            act.wait_ge(d_xt, 16)
            split_his(SPLITS[0:2])
            act.wait_ge(d_w0q, 16)
            split_his(SPLITS[2:4])
            act.wait_ge(d_xt2, 16)
            split_his(SPLITS[4:6])
            act.wait_ge(d_prm, 16)
            load_table(ACT.Sqrt)
            project_hi(0)
            ln_sqrts(0, 0)
            project_hi(1)
            project_hi(2)
            ln_sqrts(0, 1)
            for i in range(3, 6):
                project_hi(i)
            ln_his(0, 0)
            project_hi(6)
            project_hi(7)
            ln_his(0, 1)
            for i in range(8, 16):
                project_hi(i)
            act.activation(prm[:, C_GATE:C_GATE + 1], prm[:, C_GATE:C_GATE + 1], ACT.Tanh).then_inc(gate_t, 1)
            def spread_v_hi(b, g):
                for t in range(2):
                    a = act.activation(v0p_part(t, g, 0), v0_part(b, t, g), ACT.Copy)
                a.then_inc(vp_hi, 1)

            for i in range(16, 24):
                act.wait_ge(pj_mm, i + 1)
                act.activation(v0[:, i - 16, :], projected(i)[:, 0:HID], ACT.Copy).then_inc(v0_cp, 1)
                if i == 17:
                    load_table(ACT.Exp)
                    act.wait_ge(v0p_zero, 1)
                    act.wait_ge(v0_cp, 2)
                    spread_v_hi(0, 0)
            act.wait_ge(v0_cp, 8)

            def gated_batch(b, first=False, last=False):
                for k in range(HEADS + (TAIL0 if last else 0)):
                    m = k - T_LAG0
                    if (m >= 0 or not first) and m < HEADS:
                        n = b * HEADS + m
                        act.wait_ge(g_t, n + 1)
                        if not (first and m < 2):
                            act.wait_ge(g_pv, n - 1)
                        act.activation(pt0H[:, m % 2, :], bank[2 + m % 2][:, :], ACT.Copy).then_inc(g_pth, 1)
                    if k < HEADS:
                        n = b * HEADS + k
                        act.wait_ge(g_max, n + 1)
                        if not (first and k < 4):
                            act.wait_ge(g_t, n - 3)
                        for qt in range(2):
                            e = act.activation(p0[:, k % 4, qt, :], s0[:, k % 2, qt, :], ACT.Exp,
                                               bias=nb[:, k % 4, qt:qt + 1], scale=-1.0,
                                               accum_out=sm[:, k % 4, qt:qt + 1])
                        e.then_inc(g_exp, 1)
                    m = k - PV_LAG0
                    if (m >= 0 or not first) and m < HEADS and m % HG0 == HG0 - 1:
                        g = m // HG0
                        act.wait_ge(g_pv, b * HEADS + m + 1)
                        act.activation(a0H[:, g % NG0, :], bank[4 + g % 2][:, 0:SEQ], ACT.Copy).then_inc(g_ah, 1)
                    if last and k == 18:
                        load_table(ACT.Sqrt)
                    if last and k == 20:
                        ln_sqrts(1, 0)
                    if k % HG0 == 2 and k < HEADS and not (last and k == 14):
                        g = k // HG0 + 1
                        if not (first and g < NG0):
                            act.wait_ge(g_pv, b * HEADS + 4 * (g - NG0) + 4)
                        spread_v_hi(b + g // NG0, g % NG0)

            gated_batch(0, first=True)
            with act.Fori(1, BATCH - 1) as b:
                gated_batch(b)
            gated_batch(BATCH - 1, last=True)
            def body(L, j, first=False, last=False):
                for k in range(STEPS + (TAIL if last else 0)):
                    if k < STEPS:
                        act.wait_ge(s_nb, L * 64 + j * STEPS + k + 1)
                        if not (first_body(j) and k < 2):
                            act.wait_ge(t_mm, L * 64 + j * STEPS + k - 1)
                            act.wait_ge(s_pb, L * 64 + j * STEPS + k - 1)
                        for qt in range(2):
                            e = act.activation(pr[:, k % 2, qt, :], bank[qt][:, 0:TOK], ACT.Exp,
                                               bias=nb[:, k % 2, qt:qt + 1], scale=SCALE,
                                               accum_out=sm[:, k % 2, qt:qt + 1])
                        e.then_inc(s_exp, 1)
                    if k < STEPS and not (first and k < 2) and not (last and k // 2 + 1 >= STEPS // 2):
                        project_qk_hi(L, j, k // 2 + 1, k % 2 == 0)
                    if first and k == 1:
                        ln_his(L + 1, 1, (1,))
                    if last and k in (13, 17):
                        i = (k - 13) // 4
                        act.wait_ge(pbt_mm, L * 2 + i + 1)
                        act.activation(pbT[:, i * 512:(i + 1) * 512], bank[6][0:BWR, :], ACT.Copy).then_inc(pbt_cp, 1)
                    if (k >= 2 or not first) and k - 2 < STEPS:
                        m = k - 2
                        _, _, h, b = step(m)
                        act.wait_ge(pv_mm, L * 64 + j * STEPS + m + 1)
                        act.activation(aH[:, (m // 4) % 2, h, b * SEQ:(b + 1) * SEQ], bank[3][:, 0:SEQ],
                                       ACT.Copy).then_inc(a_hi, 1)
                    if (k >= 1 or not first) and k - 1 < STEPS:
                        m = k - 1
                        act.wait_ge(t_mm, L * 64 + j * STEPS + m + 1)
                        act.activation(ptH[:, m % 2, :], bank[2][:, :], ACT.Copy).then_inc(pt_hi, 1)
                    if k < STEPS and not (first and k == 0) and not (last and k + 4 >= STEPS):
                        project_v_hi(L, j, k + 4)
                    if first and k == 0:
                        ln_his(L + 1, 1, (0,))
                        project_qk_hi(L, j, 1, True)
                    if last and k == 15:
                        load_table(ACT.Sqrt)
                    if last and k == 17:
                        ln_sqrts(L + 2, 0)

            def project_v_hi(L, j, m):
                act.wait_ge(v_mm, L * 64 + j * STEPS + m + 1)
                act.activation(vH[:, (m // 4) % 2, m % 4, :], value_bank(j, m)[:, 0:GW], ACT.Copy).then_inc(v_hi, 1)

            def project_qk_hi(L, j, u, is_q):
                g, h = (u // 4) % 2, u % 2
                if is_q:
                    act.wait_ge(q_mm, L * 32 + j * 8 + u + 1)
                    act.activation(qH[:, u % 2, :], bank[4][:, :], ACT.Identity,
                                   bias=small[:, g, h:h + 1]).then_inc(q_hi, 1)
                else:
                    act.wait_ge(k_mm, L * 32 + j * 8 + u + 1)
                    act.activation(kH[:, u % 2, :, 0:SEQ], bank[5][:, :].rearrange("p (b t) -> p b t", b=2),
                                   ACT.Identity, bias=small[:, g, 2 + h:3 + h]).then_inc(k_hi, 1)

            with act.Fori(0, LAYERS) as L:
                project_v_hi(L, 0, 0)
                ln_his(L + 1, 0)
                project_v_hi(L, 0, 1)
                ln_sqrts(L + 1, 1)
                project_qk_hi(L, 0, 0, False)
                load_table(ACT.Exp)
                project_v_hi(L, 0, 2)
                project_v_hi(L, 0, 3)
                project_qk_hi(L, 0, 0, True)
                project_qk_hi(L, 0, 1, False)
                project_v_hi(L, 0, 4)
                body(L, 0, first=True)
                with act.Fori(1, BODIES - 1) as j:
                    body(L, j)
                body(L, BODIES - 1, last=True)

            ln_his(LAYERS + 1, 0)
            ln_sqrts(LAYERS + 1, 1)
            for i in range(2 * FT):
                if i == 4:
                    ln_his(LAYERS + 1, 1)
                f = i % FT
                act.wait_ge(f1_mm, i + 1)
                if i >= 2:
                    act.wait_ge(f1_lo, i - 1)
                act.activation(gel[:, i % 2, :], bank[4 + i % 2][:, :], ACT.Gelu,
                               bias=prm[:, C_B1 + f:C_B1 + f + 1]).then_inc(f1_gelu, 1)

        @block.vector
        def _(dve):
            def ln_stats(n, r, src):
                dve.bn_stats(ln_st[:, r, :], src).then_inc(ln_stat, 1)

            def ln_vars(n, half):
                h = slice(4 * half, 4 * half + 4)
                dve.wait_ge(ln_stat, n * RT + 4 * half + 4)
                dve.nop(nofuse=True)
                for r in range(4 * half, 4 * half + 4):
                    ag = dve.bn_aggr(ln_mv[:, r, :], ln_st[:, r, :])
                ag.then_inc(ln_agg, 1)
                dve.wait_ge(ln_agg, n * 4 + 2 * half + 1)
                dve.tensor_scalar(ln_sd[:, h], ln_mv[:, h, 1], EPS, None, ALU.add).then_inc(ln_agg, 1)

            def ln_norms(n, half, src):
                h = slice(4 * half, 4 * half + 4)
                dve.wait_ge(ln_sqrt, n * 2 + half + 1)
                dve.reciprocal(ln_rs[:, h], ln_sd[:, h]).then_inc(ln_rcp, 1)
                dve.wait_ge(ln_rcp, n * 2 + half + 1)
                for r in range(4 * half, 4 * half + 4):
                    dve.tensor_scalar(xn[:, r, :], src[:, r, :], ln_mv[:, r, 0:1], ln_rs[:, r:r + 1],
                                      ALU.subtract, ALU.mult).then_inc(ln_xn, 1)

            def ln_los(n, half, kts=range(KT)):
                H, Lo = (anH, anL) if first_body(n) else (hH, hL)
                for kt in kts:
                    dve.wait_ge(ln_hi, n * 4 + 2 * half + kt + 1)
                    r = slice(half * 512, half * 512 + 512)
                    dve.tensor_tensor(Lo[:, kt, r], ln_y[:, kt, :], as_f32(H[:, kt, r]),
                                      ALU.subtract).then_inc(ln_lo, 1)

            def split_los(parts, n0):
                for n, (what, c) in enumerate(parts):
                    src, hi, lo = split_aps(what, c)
                    dve.wait_ge(sp_hi, n0 + n + 1)
                    dve.tensor_tensor(lo, src, as_f32(hi), ALU.subtract).then_inc(sp_lo, 1)

            def project_lo(i):
                half, g = divmod(i % 8, NG0)
                r = slice(half * 512, half * 512 + 512)
                dve.wait_ge(pj_hi, i + 1)
                if i < 8:
                    dve.tensor_tensor(q0[64:P, g, r], projected(i)[64:P, :], q0[64:P, g, r],
                                      ALU.subtract).then_inc(pj_lo, 1)
                else:
                    dve.tensor_tensor(k0L[:, g, r], projected(i)[:, :], as_f32(k0H[:, g, r]),
                                      ALU.subtract).then_inc(pj_lo, 1)

            split_los(SPLITS, 0)
            dve.wait_ge(d_prm, 16)
            dve.wait_ge(d_crows, 16)
            for r in range(RT):
                ln_stats(0, r, c_rows[:, r, :])
                if r == 3:
                    ln_vars(0, 0)
                    project_lo(0)
            ln_vars(0, 1)
            ln_norms(0, 0, c_rows)
            project_lo(1)
            project_lo(2)
            ln_norms(0, 1, c_rows)
            for i in range(3, 6):
                project_lo(i)
            ln_los(0, 0)
            project_lo(6)
            project_lo(7)
            ln_los(0, 1)
            project_lo(8)
            project_lo(9)
            dve.wait_ge(d_mask, 16)
            dve.tensor_copy(maskb[:, :], mask8[:, :]).then_inc(mask_s, 1)
            dve.wait_ge(mask_s, 1)
            dve.tensor_scalar(maskb[:, :], maskb[:, :], 1.0, 3.0e38, ALU.subtract, ALU.mult).then_inc(mask_s, 1)
            dve.wait_ge(mask_s, 2)
            dve.tensor_scalar(maskb[:, :], maskb[:, :], 10.0, None, ALU.mult).then_inc(mask_ready, 1)
            for i in range(10, 16):
                project_lo(i)
            dve.wait_ge(mask_ready, 1)
            dve.wait_ge(d_x, 16)
            dve.wait_ge(gate_t, 1)
            dve.wait_ge(v0_cp, 8)
            def spread_v_lo(b, g):
                dve.wait_ge(vp_hi, b * NG0 + g + 1)
                for t in range(2):
                    a = dve.tensor_tensor(v0p_part(t, g, 1), v0_part(b, t, g), as_f32(v0p_part(t, g, 0)), ALU.subtract)
                a.then_inc(vp_lo, 1)

            def add_gated(row_tile, qt):
                rt = row_tile + qt
                dve.wait_ge(g_wo, rt + 1)
                rows = x[:, bass.ds(rt, 1), :].rearrange("p r c -> p (r c)")
                dve.scalar_tensor_tensor(rows, bank[6 + qt][:, 0:HID], prm[:, C_GATE:C_GATE + 1], rows,
                                         ALU.mult, ALU.add).then_inc(g_add, 1)

            def gated_batch(b, first=False, last=False):
                if not first:
                    dve.wait_ge(g_max, b * HEADS)
                dve.tensor_copy(maskc[:, :], maskb[:, bass.ds(b * SEQ, SEQ)]).then_inc(mk_cp, 1)
                dve.wait_ge(mk_cp, b + 1)
                for k in range(HEADS + (TAIL0 if last else 0)):
                    if k < HEADS:
                        n = b * HEADS + k
                        dve.wait_ge(g_s, n + 1)
                        if not (first and k < 2):
                            dve.wait_ge(g_exp, n - 1)
                        dve.nop(nofuse=True)
                        for qt in range(2):
                            t = dve.tensor_tensor_reduce(
                                out=s0[:, k % 2, qt, :], in0=bank[k % 2][:, qt * SEQ:(qt + 1) * SEQ],
                                in1=maskc[:, :], scale=-1.0, scalar=3.0e38, op0=ALU.add, op1=ALU.min,
                                accum_out=nb[:, k % 4, qt:qt + 1])
                        t.then_inc(g_max, 1)
                    m = k - 1
                    if (m >= 0 or not first) and m < HEADS:
                        n = b * HEADS + m
                        dve.wait_ge(g_exp, n + 1)
                        if not (first and m < 4):
                            dve.wait_ge(g_norm, n - 3)
                        dve.reciprocal(rs[:, m % 4, :], sm[:, m % 4, :]).then_inc(g_rs, 1)
                    m = k - PV_LAG0 - 1
                    if (m >= 0 or not first) and m < HEADS and m % HG0 == HG0 - 1:
                        g = m // HG0
                        dve.wait_ge(g_ah, b * NG0 + g + 1)
                        dve.tensor_tensor(a0L[:, g % NG0, :], bank[4 + g % 2][:, 0:SEQ], as_f32(a0H[:, g % NG0, :]),
                                          ALU.subtract).then_inc(g_al, 1)
                    m = k - T_LAG0
                    if (m >= 0 or not first) and m < HEADS:
                        dve.wait_ge(g_pth, b * HEADS + m + 1)
                        dve.tensor_tensor(pt0L[:, m % 2, :], bank[2 + m % 2][:, :], as_f32(pt0H[:, m % 2, :]),
                                          ALU.subtract).then_inc(g_ptl, 1)
                    if k % HG0 == 3 and k < HEADS and not (last and k == 15):
                        g = k // HG0 + 1
                        spread_v_lo(b + g // NG0, g % NG0)
                    if k in (12, 14) and not first:
                        add_gated(b * 2 - 2, k // 2 - 6)
                    if k == 22:
                        add_gated(b * 2, 0)
                        add_gated(b * 2, 1)
                    for rt in {16: (0, 1), 17: (2, 3), 20: (4, 5)}.get(k, ()):
                        dve.wait_ge(g_add, rt + 1)
                        ln_stats(1, rt, x[:, rt, :])
                    if last and k == 19:
                        ln_vars(1, 0)
                    if last and k == 21:
                        ln_norms(1, 0, x)

            spread_v_lo(0, 0)
            gated_batch(0, first=True)
            with dve.Fori(1, BATCH - 1) as b:
                gated_batch(b)
            gated_batch(BATCH - 1, last=True)
            for rt in (6, 7):
                dve.wait_ge(g_add, rt + 1)
                ln_stats(1, rt, x[:, rt, :])
            ln_vars(1, 1)

            def project_v_lo(L, j, m):
                dve.wait_ge(v_hi, L * 64 + j * STEPS + m + 1)
                s = (m // 4) % 2
                dve.tensor_tensor(vL[:, s, m % 4, :], value_bank(j, m)[:, 0:GW], as_f32(vH[:, s, m % 4, :]),
                                  ALU.subtract).then_inc(v_lo, 1)

            def project_qk_lo(L, j, u, is_q):
                g, h = (u // 4) % 2, u % 2
                if is_q:
                    dve.wait_ge(q_hi, L * 32 + j * 8 + u + 1)
                    dve.scalar_tensor_tensor(qL[:, u % 2, :], bank[4][:, :], small[:, g, h:h + 1],
                                             as_f32(qH[:, u % 2, :]), ALU.add, ALU.subtract).then_inc(q_lo, 1)
                else:
                    dve.wait_ge(k_hi, L * 32 + j * 8 + u + 1)
                    dve.scalar_tensor_tensor(kL[:, u % 2, :, 0:SEQ], bank[5][:, :].rearrange("p (b t) -> p b t", b=2),
                                             small[:, g, 2 + h:3 + h], as_f32(kH[:, u % 2, :, 0:SEQ]),
                                             ALU.add, ALU.subtract).then_inc(k_lo, 1)

            def add_bias_product(L, j, g, before):
                dve.wait_ge(bw_mm, L * GROUPS + j * 2 + g + 1)
                dve.tensor_tensor(bw[:, :], bank[7][0:BWR, 0:HID], before, ALU.add).then_inc(bw_add, 1)

            def add_output(L, j, m, last):
                rt = (m // 4) % 2 * 4 + m % 4
                dve.wait_ge(o_mm, L * 64 + j * STEPS + m + 1)
                dve.tensor_tensor(x[:, rt, :], output_bank(m, last)[:, 0:HID], x[:, rt, :], ALU.add).then_inc(x_add, 1)

            def final_rows(L, j, ms):
                for m in ms:
                    rt = m - 8
                    dve.wait_ge(x_add, L * 64 + j * STEPS + m + 1)
                    ln_stats(L + 2, rt, x[:, rt, :])

            def body(L, j, first=False, last=False):
                for k in range(STEPS + (TAIL + 1 if last else 0)):
                    if k < STEPS:
                        dve.wait_ge(s_mm, L * 64 + j * STEPS + k + 1)
                        for qt in range(2):
                            t = dve.tensor_reduce(mx[:, k % 2, qt:qt + 1], bank[qt][:, 0:TOK], AX_X, ALU.max)
                        t.then_inc(s_max, 1)
                        dve.wait_ge(s_max, L * 64 + j * STEPS + k + 1)
                        dve.tensor_scalar(nb[:, k % 2, :], mx[:, k % 2, :], -SCALE, None,
                                          ALU.mult).then_inc(s_nb, 1)
                    if first and k == 1:
                        project_qk_lo(L, j, 1, True)
                        ln_los(L + 1, 1, (0,))
                    if (k + 3 < STEPS or not last) and not (first and k < 2):
                        project_v_lo(L, j, k + 3)
                    for m in outputs_at(k - 1, first, last):
                        add_output(L, j, m, last)
                    if last and k > 14:
                        final_rows(L, j, outputs_at(k - 1, first, last))
                    if last and k == 18:
                        ln_norms(L + 2, 0, x)
                    if k < STEPS:
                        dve.wait_ge(s_exp, L * 64 + j * STEPS + k + 1)
                        dve.reciprocal(rs[:, k % 2, :], sm[:, k % 2, :]).then_inc(s_rs, 1)
                    if k < STEPS and k % 8 == 0 and not (first and k == 0):
                        add_bias_product(L, j, k // 8, bw[:, :])
                    if k < STEPS and not (first and k < 2) and not (last and k // 2 + 1 >= STEPS // 2):
                        project_qk_lo(L, j, k // 2 + 1, k % 2 == 0)
                    if first and k == 1:
                        ln_los(L + 1, 1, (1,))
                    if (k >= 2 or not first) and k - 2 < STEPS:
                        m = k - 2
                        _, _, h, b = step(m)
                        dve.wait_ge(a_hi, L * 64 + j * STEPS + m + 1)
                        t = slice(b * SEQ, (b + 1) * SEQ)
                        dve.tensor_tensor(aL[:, (m // 4) % 2, h, t], bank[3][:, 0:SEQ],
                                          as_f32(aH[:, (m // 4) % 2, h, t]), ALU.subtract).then_inc(a_lo, 1)
                    if (k >= 1 or not first) and k - 1 < STEPS:
                        m = k - 1
                        dve.wait_ge(pt_hi, L * 64 + j * STEPS + m + 1)
                        dve.tensor_tensor(ptL[:, m % 2, :], bank[2][:, :], as_f32(ptH[:, m % 2, :]),
                                          ALU.subtract).then_inc(pt_lo, 1)
                    if last and k == 17:
                        ln_vars(L + 2, 0)

            dve.wait_ge(d_bo, 16)
            with dve.Fori(0, LAYERS) as L:
                project_v_lo(L, 0, 0)
                ln_los(L + 1, 0)
                project_v_lo(L, 0, 1)
                project_qk_lo(L, 0, 0, False)
                ln_norms(L + 1, 1, x)
                project_v_lo(L, 0, 2)
                project_v_lo(L, 0, 3)
                project_qk_lo(L, 0, 0, True)
                project_qk_lo(L, 0, 1, False)
                add_bias_product(L, 0, 0, bo[:, L, :])
                project_v_lo(L, 0, 4)
                body(L, 0, first=True)
                with dve.Fori(1, BODIES - 1) as j:
                    body(L, j)
                body(L, BODIES - 1, last=True)
                ln_vars(L + 2, 1)

            ln_los(LAYERS + 1, 0)
            ln_norms(LAYERS + 1, 1, x)
            dve.wait_ge(d_b2, 16)
            for i in range(2 * FT):
                if i == 4:
                    ln_los(LAYERS + 1, 1)
                if 6 <= i < 6 + RT:
                    dve.tensor_tensor(x[:, i - 6, :], x[:, i - 6, :], b2b[:, :], ALU.add).then_inc(m_xb, 1)
                half, f = divmod(i, FT)
                r = slice(half * 512, half * 512 + 512)
                dve.wait_ge(f1_gelu, i + 1)
                dve.tensor_copy(gH[:, f, r], gel[:, i % 2, :]).then_inc(f1_hi, 1)
                dve.wait_ge(f1_hi, i + 1)
                dve.tensor_tensor(gL[:, f, r], gel[:, i % 2, :], as_f32(gH[:, f, r]), ALU.subtract).then_inc(f1_lo, 1)
            dve.wait_ge(m_xb, RT)
            for r in range(RT):
                dve.wait_ge(f2_mm, r + 1)
                dve.tensor_tensor(res[:, r, :], bank[6 + r % 2][:, 0:HID], x[:, r, :], ALU.add).then_inc(f2_add, 1)

        @block.gpsimd
        def _(pool):
            def split(src, hi, lo, count, hi_sem, lo_sem):
                pool.tensor_scalar(hi, src, 1.0, 1.0, ALU.mult, ALU.mult).then_inc(hi_sem, 1)
                pool.wait_ge(hi_sem, count)
                pool.nop(nofuse=True)
                return pool.tensor_tensor(lo, src, as_f32(hi), ALU.subtract).then_inc(lo_sem, 1)

            pool.wait_ge(d_w0, 16)
            pool.nop(nofuse=True)
            for i in range(5):
                c = slice(C0_K + i * 512, C0_K + (i + 1) * 512)
                split(w0raw[:, c], w0H[:, c], w0L[:, c], i + 1, c_hi, c_lo)
            pool.wait_ge(d_ct, 16)
            pool.nop(nofuse=True)
            for i in range(4):
                kt, r = divmod(i * 512, ROWS)
                split(ct_raw[:, i * 512:(i + 1) * 512], ctxH[:, kt, r:r + 512], ctxL[:, kt, r:r + 512],
                      i + 6, c_hi, c_lo)
            pool.wait_ge(pj_mm, 8)
            pool.nop(nofuse=True)
            for t in range(2):
                z = pool.memset(as_f32(v0p[t]), 0.0)
            z.then_inc(v0p_zero, 1)

            def masked_q(b, k):
                pool.tensor_tensor(q0m[:, k % 4, :], q0[:, k // HG0, bass.ds(b * SEQ, SEQ)],
                                   prm[:, C_MASK + k % HG0:C_MASK + k % HG0 + 1].to_broadcast([P, SEQ]),
                                   ALU.mult).then_inc(g_qm, 1)

            def gated_batch(b, first=False, last=False):
                for k in range(HEADS + (1 if last else 0)):
                    if k < HEADS and not (last and k + 2 >= HEADS):
                        if not (first and k < 2):
                            pool.wait_ge(g_s, b * HEADS + k - 1)
                            pool.nop(nofuse=True)
                        masked_q(b + (k + 2) // HEADS, (k + 2) % HEADS)
                    m = k - 1
                    if m >= 0 or not first:
                        pool.wait_ge(g_rs, b * HEADS + m + 1)
                        pool.nop(nofuse=True)
                        for qt in range(2):
                            t = pool.tensor_scalar(p0[:, m % 4, qt, :], p0[:, m % 4, qt, :], rs[:, m % 4, qt:qt + 1],
                                                   1.0, ALU.mult, ALU.mult)
                        t.then_inc(g_norm, 1)

            def split_v(n, g):
                pool.wait_ge(d_wa, n * 16 + 16)
                pool.nop(nofuse=True)
                pool.tensor_copy(small[:, g, :], stage[:, C_SMALL:C_O])
                split(stage[:, C_SMALL + 4:C_O], kbH[:, g, :], kbL[:, g, :], n * 6 + 1, w_hi, w_hi_b)
                split(stage[:, C_V:C_Q], wH[g][:, 0:512], wL[g][:, 0:512], n * 6 + 2, w_hi, w_v)

            def split_q(n, g):
                split(stage[:, C_Q:C_K], wH[g][:, 512:1024], wL[g][:, 512:1024], n * 6 + 3, w_hi, w_q)

            def split_k(n, g):
                split(stage[:, C_K:C_SMALL], wH[g][:, 1024:1536], wL[g][:, 1024:1536], n * 6 + 4, w_hi, w_k)

            def split_o(n, g):
                pool.wait_ge(d_wo, n * 16 + 16)
                pool.nop(nofuse=True)
                pool.tensor_tensor(bv[:, :], stage[:, C_BV:C_BV + GH * BWR], stage[:, C_BV + GH * BWR:C_END],
                                   ALU.subtract).then_inc(bv_d, 1)
                pool.wait_ge(bv_d, n + 1)
                pool.nop(nofuse=True)
                split(bv[:, :], bvH[:, g, :], bvL[:, g, :], n * 6 + 5, w_hi, w_hi_b)
                split(stage[:, C_O:C_BV], wH[g][:, 1536:2048], wL[g][:, 1536:2048], n * 6 + 6, w_hi, w_o)

            pool.wait_ge(sp_lo, 6)
            pool.wait_ge(pj_lo, 8)
            pool.nop(nofuse=True)
            masked_q(0, 0)
            masked_q(0, 1)
            gated_batch(0, first=True)
            with pool.Fori(1, BATCH - 1) as b:
                gated_batch(b)
            gated_batch(BATCH - 1, last=True)
            split_v(0, 0)
            split_q(0, 0)
            split_k(0, 0)
            split_o(0, 0)

            pool.wait_ge(g_add, 2 * BATCH)
            pool.nop(nofuse=True)
            pool.memset(pb[:, :, HEADS:BWR], 1.0).then_inc(pb_ones, 1)

            def key_bias(L, j, u):
                g, h = (u // 4) % 2, u % 2
                pool.wait_ge(w_hi_b, L * GROUPS * 2 + j * 4 + (u // 4) * 2 + 1)
                pool.nop(nofuse=True)
                if not (first_body(j) and u < 2):
                    pool.wait_ge(s_mm, L * 64 + j * STEPS + 2 * (u - 1))
                pool.nop(nofuse=True)
                for dst, src in ((kH, kbH), (kL, kbL)):
                    t = pool.tensor_copy(dst[:, u % 2, :, SEQ:KW], as_r(src, g, h))
                t.then_inc(kb_cp, 1)

            def as_r(src, g, h):
                return src[:, g, h:h + 1].unsqueeze(2).to_broadcast([P, 2, 2])

            def body(L, j, first=False, last=False):
                for k in range(STEPS):
                    if k % 2 == 0 and not (last and k // 2 + 1 >= STEPS // 2):
                        key_bias(L, j, k // 2 + 1)
                    slot, bp, h, b = step(k)
                    pool.wait_ge(s_rs, L * 64 + j * STEPS + k + 1)
                    pool.nop(nofuse=True)
                    for qt in range(2):
                        t = pool.tensor_scalar(pr[:, k % 2, qt, :], pr[:, k % 2, qt, :], rs[:, k % 2, qt:qt + 1], 1.0,
                                               ALU.mult, ALU.mult)
                    t.then_inc(s_norm, 1)
                    pool.wait_ge(s_norm, L * 64 + j * STEPS + k + 1)
                    pool.nop(nofuse=True)
                    rt = (bp * 2 + b) * 2
                    head = j * 4 + slot * 2 + h
                    pool.tensor_copy(pb[:, rt:rt + 2, bass.ds(head, 1)], pr[:, k % 2, :, SEQ:TOK]).then_inc(s_pb, 1)
                    g = k // 8
                    n = L * GROUPS + j * 2 + g + 1
                    if k % 8 == 0:
                        split_v(n, (g + 1) % 2)
                    if k % 8 == 1:
                        split_q(n, (g + 1) % 2)
                    if k % 8 == 2:
                        split_k(n, (g + 1) % 2)
                    if k % 8 == 6:
                        split_o(n, (g + 1) % 2)

            with pool.Fori(0, LAYERS) as L:
                key_bias(L, 0, 0)
                body(L, 0, first=True)
                with pool.Fori(1, BODIES - 1) as j:
                    body(L, j)
                body(L, BODIES - 1, last=True)

            pool.wait_ge(d_w2, 16)
            pool.nop(nofuse=True)
            for i in range(4):
                c = slice(i * 512, (i + 1) * 512)
                split(w2raw[:, c], w2H[:, c], w2L[:, c], i + 1, m_whi, m_w)


def _by_partition(a):
    n = a.shape[0] // P
    return np.ascontiguousarray(a.reshape(n, P, a.shape[1]).transpose(1, 0, 2)).reshape(P, -1)


def _layout(i):
    f = {k: np.asarray(v) for k, v in i.items()}
    x_rows = f["x"].reshape(ROWS, HID)
    ctx_rows = f["ctx_2048"].reshape(ROWS, HID)
    pre = "L1_xattn_"

    cols = []
    for g, b in (("L0_xattn_ln_gamma", "L0_xattn_ln_beta"), (pre + "ln1_scale", pre + "ln1_offset"),
                 (pre + "ln2_scale", pre + "ln2_offset"), (pre + "ln_mlp_scale", pre + "ln_mlp_offset")):
        cols += [f[g].reshape(KT, P).T, f[b].reshape(KT, P).T]
    cols.append(np.broadcast_to(f["L0_xattn_gate"].reshape(1, 1), (P, 1)))
    cols.append(f[pre + "b_fc1"].reshape(FT, P).T)
    own = (np.arange(P)[:, None] // HD0) % HG0 == np.arange(HG0)[None, :]
    cols.append(np.where(own, np.float32(SCALE0), np.float32(0)))
    cols = np.ascontiguousarray(np.concatenate(cols, axis=1))

    def twice(w):
        t = w.T.reshape(KT, P, NG0, 1, HG0 * HD0)
        return np.broadcast_to(t, (KT, P, NG0, 2, HG0 * HD0)).transpose(1, 0, 2, 3, 4).reshape(P, -1)

    wo = f["L0_xattn_Wo"].T.reshape(NG0, HG0, 1, HD0, HID)
    wo = np.broadcast_to(wo, (NG0, HG0, 2, HD0, HID)).transpose(1, 2, 3, 0, 4).reshape(P, -1)
    w0 = np.ascontiguousarray(np.concatenate(
        [twice(f["L0_xattn_Wq"]), twice(f["L0_xattn_Wk"]), _by_partition(f["L0_xattn_Wv"].T), wo], axis=1))

    wg = np.zeros((LAYERS, GROUPS, P, C_END), np.float32)
    bo18 = np.zeros((BWR, LAYERS, HID), np.float32)
    for n in range(LAYERS):
        get = lambda name: f[f"{pre}{name}{n + 1}"]
        for g in range(GROUPS):
            w = wg[n, g]
            s = slice(g * GW, (g + 1) * GW)
            for c, name in ((C_V, "wv"), (C_Q, "wq"), (C_K, "wk")):
                w[:, c:c + 512] = _by_partition(get(name)[:, s])
            w[:, C_O:C_BV] = _by_partition(get("wo")[s])
            for h in range(GH):
                head = g * GH + h
                d = slice(head * HD, (head + 1) * HD)
                w[:, C_SMALL + h] = get("bq")[d]
                w[:, C_SMALL + 2 + h] = get("bk")[d]
                w[:, C_SMALL + 4 + h] = get("bias_k")[0, 0, head]
                a, b = C_BV + h * BWR, C_BV + (GH + h) * BWR
                w[:, a + head] = get("bias_v")[0, 0, head]
                w[:, a + HEADS] = get("bv")[d]
                w[:, b + head] = get("bv")[d]
        bo18[HEADS + 1, n] = get("bo")
    w1 = _by_partition(f[pre + "w_fc1"])
    wg = wg.reshape(LAYERS * GROUPS, P, C_END)
    tail = np.zeros((1, P, C_END), np.float32)
    tail[0, :, 0:C_SMALL] = w1[:, 0:C_SMALL]
    tail[0, :, C_O:C_BV] = w1[:, C_SMALL:]
    wg = np.concatenate([wg, tail])
    mask = f["mask_BxS2_bf1"].reshape(1, ROWS).view(np.uint8)
    return {
        "x_rows": x_rows, "x_t": _by_partition(x_rows.T), "ctx_rows": ctx_rows, "ctx_t": _by_partition(ctx_rows.T),
        "mask_rows": np.ascontiguousarray(np.broadcast_to(mask, (P, ROWS))), "cols": cols,
        "ident_in": np.eye(P, dtype=np.float32), "w0": w0, "wg": wg, "bo18": bo18,
        "w2": _by_partition(f[pre + "w_fc2"]),
        "b2": np.ascontiguousarray(np.broadcast_to(f[pre + "b_fc2"].reshape(1, HID), (P, HID))),
    }


def kernel(**inputs):
    import concourse.bacc as bacc
    from concourse.bass_utils import run_bass_kernel_spmd

    nc = bacc.Bacc("TRN2", target_bir_lowering=False, num_devices=1)
    arrays, args = {}, {}
    for name, a in _layout(inputs).items():
        a = np.ascontiguousarray(a)
        arrays[name] = a
        args[name] = nc.dram_tensor(name, a.shape, mybir.dt.from_np(a.dtype), kind="ExternalInput").ap()
    out = nc.dram_tensor("out", (ROWS, HID), F32, kind="ExternalOutput").ap()
    build_program(nc, **args, out=out)
    r = run_bass_kernel_spmd(nc, [arrays], core_ids=[0])
    return r.results[0]["out"].reshape(BATCH, SEQ, HID)
```
